# Optimizing a Trainium2 kernel written in Bass

```python
import numpy as np
import jax
import jax.numpy as jnp

def _softmax(x, axis=-1):
    return jax.nn.softmax(x, axis=axis)

def _gelu(x):
    return jax.nn.gelu(x, approximate=True)

def _silu(x):
    return jax.nn.silu(x)

def _sigmoid(x):
    return jax.nn.sigmoid(x)

def _layernorm(x, axis=-1, eps=1e-05):
    m = jnp.mean(x, axis=axis, keepdims=True)
    v = jnp.var(x, axis=axis, keepdims=True)
    return (x - m) / jnp.sqrt(v + eps)

def _scatter_add(tgt, idx, src, axis=0):
    return tgt.at[idx].add(src)

def _segment_sum(src, seg, n):
    return jax.ops.segment_sum(src, seg, n)
kernel_name = 'mk_seq_preln_d1_jaxref_r8_dc0886'

def setup_inputs(seed: int=0):
    np.random.seed(seed)
    _w = jnp.asarray

    def _L0_attn_setup():
        import jax, jax.numpy as jnp
        import numpy as np
        B, L, D = (2, 256, 128)
        H, HD = (16, 64)
        LD = 32
        key = jax.random.key(seed)
        ks = jax.random.split(key, 6)
        s = lambda fan_in: 1.0 / np.sqrt(fan_in)
        x_bld = jax.random.normal(ks[0], (B, L, D), dtype=jnp.float32)
        Wq = jax.random.normal(ks[1], (D, H, HD), dtype=jnp.float32) * s(D)
        Wkv_down = jax.random.normal(ks[2], (D, LD), dtype=jnp.float32) * s(D)
        Wk_up = jax.random.normal(ks[3], (LD, H, HD), dtype=jnp.float32) * s(LD)
        Wv_up = jax.random.normal(ks[4], (LD, H, HD), dtype=jnp.float32) * s(LD)
        Wout = jax.random.normal(ks[5], (H, HD, D), dtype=jnp.float32) * s(H * HD)
        return {'x_bld': x_bld, 'Wq': Wq, 'Wkv_down': Wkv_down, 'Wk_up': Wk_up, 'Wv_up': Wv_up, 'Wout': Wout}
    _L0_attn_in = _L0_attn_setup()

    def _L0_ffn_setup():
        import jax, jax.numpy as jnp
        import numpy as np
        TEMPERATURE = 0.5
        CAPACITY_FACTOR = 1.25
        TOP_K = 1
        key = jax.random.key(seed)
        ks = jax.random.split(key, 5)
        B, S, D, H, E = (4, 256, 128, 256, 8)
        s = 0.02
        return {'x': jax.random.normal(ks[0], (B, S, D), jnp.float32), 'gate_w': jax.random.normal(ks[1], (E, D), jnp.float32) * s, 'gate_b': jnp.zeros((E,), jnp.float32), 'rms_w': jnp.ones((E,), jnp.float32), 'w1': jax.random.normal(ks[2], (E, D, H), jnp.float32) * s, 'b1': jnp.zeros((E, H), jnp.float32), 'w2': jax.random.normal(ks[3], (E, H, D), jnp.float32) * s, 'b2': jnp.zeros((E, D), jnp.float32)}
    _L0_ffn_in = _L0_ffn_setup()
    _d = {'L0_attn_x_bld': _L0_attn_in['x_bld'], 'L0_attn_Wq': _L0_attn_in['Wq'], 'L0_attn_Wkv_down': _L0_attn_in['Wkv_down'], 'L0_attn_Wk_up': _L0_attn_in['Wk_up'], 'L0_attn_Wv_up': _L0_attn_in['Wv_up'], 'L0_attn_Wout': _L0_attn_in['Wout'], 'L0_ffn_gate_w': _L0_ffn_in['gate_w'], 'L0_ffn_gate_b': _L0_ffn_in['gate_b'], 'L0_ffn_rms_w': _L0_ffn_in['rms_w'], 'L0_ffn_w1': _L0_ffn_in['w1'], 'L0_ffn_b1': _L0_ffn_in['b1'], 'L0_ffn_w2': _L0_ffn_in['w2'], 'L0_ffn_b2': _L0_ffn_in['b2']}
    _x0 = _d['L0_attn_x_bld']
    _d['L0_attn_x_bld'] = jax.random.normal(jax.random.fold_in(jax.random.key(seed), 1), (32, 256, 128), dtype=_x0.dtype)
    del _x0
    return _d

def reference(L0_attn_x_bld, L0_attn_Wq, L0_attn_Wkv_down, L0_attn_Wk_up, L0_attn_Wv_up, L0_attn_Wout, L0_ffn_gate_w, L0_ffn_gate_b, L0_ffn_rms_w, L0_ffn_w1, L0_ffn_b1, L0_ffn_w2, L0_ffn_b2):

    def _L0_attn_ref(x_bld, Wq, Wkv_down, Wk_up, Wv_up, Wout):
        import jax, jax.numpy as jnp
        import numpy as np
        B, L, D = (2, 256, 128)
        H, HD = (16, 64)
        LD = 32
        q_blhd = jnp.einsum('bld,dhk->blhk', x_bld, Wq)
        latent_bll = jnp.einsum('bld,dc->blc', x_bld, Wkv_down)
        k_blhd = jnp.einsum('blc,chk->blhk', latent_bll, Wk_up)
        v_blhd = jnp.einsum('blc,chk->blhk', latent_bll, Wv_up)
        attn = jnp.einsum('bqhd,bkhd->bhqk', q_blhd, k_blhd) / jnp.sqrt(jnp.asarray(HD, dtype=x_bld.dtype))
        l = x_bld.shape[1]
        mask = (jnp.arange(l)[None, :] <= jnp.arange(l)[:, None])[None, None]
        neg_inf = jnp.finfo(attn.dtype).min
        attn = jax.nn.softmax(jnp.where(mask, attn, neg_inf), axis=-1)
        y_blhd = jnp.einsum('bhqk,bkhd->bqhd', attn, v_blhd)
        return jnp.einsum('bqhd,hdo->bqo', y_blhd, Wout)

    def _L0_ffn_ref(x, gate_w, gate_b, rms_w, w1, b1, w2, b2):
        import jax, jax.numpy as jnp
        import numpy as np
        TEMPERATURE = 0.5
        CAPACITY_FACTOR = 1.25
        TOP_K = 1
        B, S, D = x.shape
        E = gate_w.shape[0]
        xf = x.reshape(-1, D)
        N = xf.shape[0]
        logits = xf @ gate_w.T + gate_b
        eps = jnp.finfo(logits.dtype).eps
        ms = jnp.mean(logits * logits, axis=-1, keepdims=True)
        logits = logits * jax.lax.rsqrt(ms + eps) * rms_w
        gates = jax.nn.softmax(logits / TEMPERATURE, axis=-1)
        g, idx = jax.lax.top_k(gates, TOP_K)
        g, idx = (g[:, 0], idx[:, 0])
        capacity = min(int(np.ceil(N * TOP_K / E * CAPACITY_FACTOR)), N)
        counts = jnp.zeros((E,), jnp.int32).at[idx].add(1)
        active = (counts > 0) & (capacity >= 1)
        mask = active[idx].astype(gates.dtype)
        masked = g * mask
        norm_g = masked / (masked + 1e-06)
        h = jax.nn.gelu(jnp.einsum('nd,edh->neh', xf, w1) + b1, approximate=False)
        y = jnp.einsum('neh,ehd->ned', h, w2) + b2
        out = (y * norm_g[:, None, None]).sum(axis=1)
        return out.reshape(B, S, D)
    x = L0_attn_x_bld
    x = x + _L0_attn_ref(_layernorm(x, axis=-1), L0_attn_Wq, L0_attn_Wkv_down, L0_attn_Wk_up, L0_attn_Wv_up, L0_attn_Wout)
    x = x + _L0_ffn_ref(_layernorm(x, axis=-1), L0_ffn_gate_w, L0_ffn_gate_b, L0_ffn_rms_w, L0_ffn_w1, L0_ffn_b1, L0_ffn_w2, L0_ffn_b2)
    return x

_drawn_inputs = setup_inputs


def setup_inputs(seed=0):
    import zlib

    import numpy as np

    out = dict(_drawn_inputs(seed))
    spreads = {'L0_ffn_gate_b': (0.0, 0.1),
     'L0_ffn_rms_w': (1.0, 0.2),
     'L0_ffn_b1': (0.0, 0.1),
     'L0_ffn_b2': (0.0, 0.1)}
    factors = {}
    for name, (base, spread) in spreads.items():
        noise = np.random.default_rng([zlib.crc32(name.encode()), seed]).standard_normal(out[name].shape)
        drawn = base * np.exp(spread * noise) if base else spread * noise
        out[name] = jnp.asarray(drawn.astype(out[name].dtype))
    for name, factor in factors.items():
        out[name] = (out[name] * factor).astype(out[name].dtype)
    return out
```

```python
import concourse.bass as bass
from concourse import mybir
from contextlib import ExitStack



def preln_block(nc, x, Wq, Wkv, Wk_up, Wv_up, Wout, gate_w, gate_b, rms_w, w1, b1, w2, b2, out):
    F32, F32R, BF16 = mybir.dt.float32, mybir.dt.float32r, mybir.dt.bfloat16
    ALU, ACT, AX = mybir.AluOpType, mybir.ActivationFunctionType, mybir.AxisListType

    B, L, D = x.shape
    _, H, HD = Wq.shape
    C = Wkv.shape[1]
    E, _, FH = w1.shape
    P = 128
    G = P // C
    NG = H // G
    QT = L // P
    NT = B * QT
    NBUF = 3
    PR = 6
    HC = E * FH // P
    CH = 512
    CT = CH // P
    NC = NT // CT
    EPS = 1e-5
    MASKED = -1.0e30
    KS = 3 * C
    PG = G * L + G * P
    assert QT == 2 and D == P and B % NBUF == 2

    x_tiles = x.rearrange("b (s p) d -> p (b s) d", p=P)
    out_tiles = out.rearrange("b (s p) d -> p (b s) d", p=P)

    keep = ExitStack()
    with keep:
        def sem(name):
            return keep.enter_context(nc.semaphore(name))

        def sb(name, shape, dt=F32, ctx=keep):
            return ctx.enter_context(nc.sbuf_tensor(name, shape, dt))

        X = sb("X", [P, NT, D])
        stats = sb("stats", [P, NT, 6])
        mv = sb("mv", [P, NT, 2])
        std = sb("std", [P, NT])
        rstd = sb("rstd", [P, NT])
        ident = sb("ident", [P, P])
        w1_raw = sb("w1_raw", [P, E, FH])
        w2_sb = sb("w2_sb", [P, HC, D])
        eps_col = sb("eps_col", [P, 1])
        banks = [keep.enter_context(nc.psum_tensor(f"bank{i}", [P, 512], F32)) for i in range(2)]
        SA = keep.enter_context(nc.psum_tensor("scores_q", [P, 3, 512], F32))
        SB_ = keep.enter_context(nc.psum_tensor("scores_k", [P, 3, 512], F32))

        with ExitStack() as a:
            Qs = [sb(f"Qstack{i}", [P, H, L], F32R, a) for i in range(NBUF)]
            Ls = [sb(f"Lstack{i}", [P, L], F32R, a) for i in range(NBUF)]
            Ln = [sb(f"latent{i}", [P, QT, C], F32, a) for i in range(NBUF)]
            Pr = [sb(f"probs{i}", [P, PG], F32, a) for i in range(PR)]
            xn = sb("xn", [P, QT, D], F32, a)
            xnT = sb("xnT", [P, L], F32, a)
            q_hi = sb("q_hi", [P, NG, L], F32R, a)
            q_lo = sb("q_lo", [P, NG, L], F32R, a)
            nmax = sb("nmax", [P, H, QT], F32, a)
            m_hi = sb("m_hi", [H * QT, P], F32R, a)
            m_lo = sb("m_lo", [H * QT, P], F32R, a)
            O = sb("O", [P, NG, L], F32, a)
            On = sb("On", [P, NG, L], F32, a)
            rden = sb("rden", [P, L], F32, a)
            rdb = sb("rdb", [P, NG, L], F32, a)
            wq_sb = Pr[0][:, 0:H * HD]
            wk_sb = Pr[1][0:C, 0:H * HD]
            wv_sb = Pr[2][0:C, 0:H * HD]
            wo_sb = Pr[3][:, 0:H * HD].rearrange("p (g o) -> p g o", o=D)
            wqT = Pr[4][:, 0:H * HD].rearrange("p (g d) -> p g d", d=D)
            wkvT = Pr[5][:, 0:H * C].rearrange("p (v g c) -> p v g c", v=2, c=C)
            wlat = sb("wlat", [P, 3, C], F32, a)
            A = sb("A", [P, H, C], F32, a)
            Wvo = sb("Wvo", [P, NG, D], F32, a)
            ident_b = sb("ident_b", [P, P], BF16, a)
            mask = sb("mask", [P, G, P], BF16, a)
            one_t = sb("one_t", [P, NG, C], F32, a)

            x_in = [sem(f"x_in{i}") for i in range(4)]
            wq_in, wk_in, wo_in, lat_in, ffn_in = sem("wq_in"), sem("wk_in"), sem("wo_in"), sem("lat_in"), sem("ffn_in")
            consts, zeroed = sem("consts"), sem("zeroed")
            masks_set, ones_set, selects_begun, shuffles_begun = sem("masks_set"), sem("ones_set"), sem("selects_begun"), sem("shuffles_begun")
            wT_ready, wT_copied, Awvo_ready, Awvo_copied = sem("wT_ready"), sem("wT_copied"), sem("Awvo_ready"), sem("Awvo_copied")
            stats_step, std_done, rstd_done = sem("stats_step"), sem("std_done"), sem("rstd_done")
            xn_ready, xT_ready, xT_copied = sem("xn_ready"), sem("xT_ready"), sem("xT_copied")
            prep_ready, hi_done, lo_done = sem("prep_ready"), sem("hi_done"), sem("lo_done")
            q_stacked = [sem(f"q_stacked{i}") for i in range(NBUF)]
            m_stacked = [sem(f"m_stacked{i}") for i in range(NBUF)]
            scores_ready, max_done = sem("scores_ready"), sem("max_done")
            mT_ready, mhi_done, m_done = sem("mT_ready"), sem("mhi_done"), sem("m_done")
            scoresT_ready, exp_done, masked = sem("scoresT_ready"), sem("exp_done"), sem("masked")
            o_ready, o_copied, d_ready, rden_done, rdb_done = sem("o_ready"), sem("o_copied"), sem("d_ready"), sem("rden_done"), sem("rdb_done")
            on_done, out_ready, x1_done, stats2_done = sem("on_done"), sem("out_ready"), sem("x1_done"), sem("stats2_done")

            def batches(eng, step):
                for u in range(NBUF):
                    step(u, 0, u, True, True)
                with eng.Fori(1, B // NBUF) as r:
                    for u in range(NBUF):
                        step(r * NBUF + u, r, u, True, True)
                for i in range(B - 2, B):
                    step(i, i // NBUF, i % NBUF, i + 1 < B, False)

            def later(b, k):
                return not isinstance(b, int) or b >= k

            def turn(r, u, k):
                return r + (u + k) // NBUF, (u + k) % NBUF

            with nc.Block() as block:
                @block.sync
                def _(sp):
                    sp.dma_start(wq_sb, Wq.rearrange("d h k -> d (h k)")).then_inc(wq_in, 16)
                    sp.dma_start(wk_sb, Wk_up.rearrange("c h k -> c (h k)")).then_inc(wk_in, 16)
                    sp.dma_start(wv_sb, Wv_up.rearrange("c h k -> c (h k)")).then_inc(wk_in, 16)
                    sp.dma_start(X[:, 0:16, :], x_tiles[:, 0:16, :]).then_inc(x_in[0], 16)
                    sp.dma_start(wo_sb, Wout.rearrange("(g a) k o -> (a k) g o", a=2)).then_inc(wo_in, 16)
                    for n in range(1, 4):
                        sp.dma_start(X[:, 16 * n:16 * n + 16, :], x_tiles[:, 16 * n:16 * n + 16, :]).then_inc(x_in[n], 16)
                    sp.dma_start(w1_raw[:, :, :], w1.rearrange("e d f -> d e f")).then_inc(ffn_in, 16)
                    sp.dma_start(w2_sb[:, :, :], w2.rearrange("e (a p) d -> p (e a) d", p=P)).then_inc(ffn_in, 16)

                    def stack_q(b, r, u):
                        sp.wait_ge(lo_done, b + 1)
                        for j in range(G):
                            for k, src in enumerate((q_hi, q_lo, q_hi)):
                                sp.dma_start(Qs[u][k * C:(k + 1) * C, j::G, :].bitcast(F32),
                                             src[j * C:(j + 1) * C, :, :].bitcast(F32)).then_inc(q_stacked[u], 16)

                    def stack_m(b, r, u):
                        sp.wait_ge(m_done, b + 1)
                        for k, src in enumerate((m_hi, m_lo)):
                            sp.dma_start(Qs[u][KS + k:KS + k + 1, :, :].rearrange("o h (s q) -> o (h s) q", q=P).bitcast(F32),
                                         src[:, :].bitcast(F32)).then_inc(m_stacked[u], 16)

                    stack_q(0, 0, 0)
                    stack_q(1, 0, 1)
                    stack_m(0, 0, 0)

                    def step(i, r, u, more, more2):
                        if more:
                            stack_m(i + 1, *turn(r, u, 1))
                        if more2:
                            stack_q(i + 2, *turn(r, u, 2))
                    batches(sp, step)
                    sp.wait_ge(ffn_in, 32)

                @block.gpsimd
                def _(pool):
                    pool.memset(ident[:, :], 0.0).then_inc(zeroed, 1)
                    pool.memset(mask[:, :, :], 0.0).then_inc(zeroed, 1)
                    pool.memset(one_t[:, :, :], 1.0).then_inc(zeroed, 1)
                    pool.memset(eps_col[:, :], EPS).then_inc(zeroed, 1)
                    pool.wait_ge(zeroed, 4)
                    pool.affine_select(out=ident[:, :], in_=ident[:, :], compare_op=ALU.not_equal, fill=1.0, base=0,
                                       pattern=[[-1, P]], channel_multiplier=1).then_inc(consts, 1)
                    pool.affine_select(out=mask[:, :, :], in_=mask[:, :, :], compare_op=ALU.is_ge, fill=MASKED, base=0,
                                       pattern=[[0, G], [-1, P]], channel_multiplier=1).then_inc(consts, 1)
                    W = C // NG
                    pool.affine_select(out=one_t[:, :, :], in_=one_t[:, :, :], compare_op=ALU.is_ge, fill=0.0, base=0,
                                       pattern=[[-W, NG], [1, C]], channel_multiplier=0).then_inc(masks_set, 1)
                    pool.wait_ge(masks_set, 1)
                    pool.affine_select(out=one_t[:, :, :], in_=one_t[:, :, :], compare_op=ALU.is_ge, fill=0.0, base=W - 1,
                                       pattern=[[W, NG], [-1, C]], channel_multiplier=0).then_inc(consts, 1)
                    pool.wait_ge(consts, 3)
                    pool.tensor_copy(ident_b[:, :], ident[:, :]).then_inc(consts, 1)

                    def mask_probs(b, t, r, u):
                        g = (4 * u + t) % PR
                        pool.wait_ge(exp_done, NG * b + t + 1)
                        pool.sem_inc(selects_begun, 1)
                        low = Pr[g][:, 0:G * L].rearrange("p (j q) -> p j q", q=L)[:, :, 0:P]
                        high = Pr[g][:, G * L:PG].rearrange("p (j q) -> p j q", q=P)
                        for part in (low, high):
                            ins = pool.affine_select(out=part, in_=part, compare_op=ALU.is_ge, fill=0.0, base=0,
                                                     pattern=[[0, G], [1, P]], channel_multiplier=-1)
                        ins.then_inc(masked, 1)

                    def divide(b):
                        pool.wait_ge(o_copied, NG * b + NG)
                        pool.wait_ge(rdb_done, b + 1)
                        if later(b, 1):
                            pool.wait_ge(out_ready, b)
                        pool.tensor_tensor(On[:, :, :], O[:, :, :], rdb[:, :, :], ALU.mult).then_inc(on_done, 1)

                    def step(i, r, u, more, more2):
                        for t in range(NG):
                            mask_probs(i, t, r, u)
                            if t == 0 and later(i, 1):
                                divide(i - 1)
                    batches(pool, step)
                    divide(B - 1)

                @block.scalar
                def _(act):
                    act.dma_start(wlat[:, 0, :], Wkv).then_inc(lat_in, 16)
                    act.dma_start(wlat[:, 1, :], Wkv).then_inc(lat_in, 16)
                    act.dma_start(wlat[:, 2, :], Wkv).then_inc(lat_in, 16)
                    act.wait_ge(wT_ready, 1)
                    act.activation(wqT, SB_[:, 0:2, :].rearrange("p a (g d) -> p (a g) d", d=D), ACT.Copy).then_inc(wT_copied, 1)
                    act.activation(wkvT, SB_[:, 2, :].rearrange("p (v g c) -> p v g c", v=2, c=C), ACT.Copy).then_inc(wT_copied, 1)
                    act.wait_ge(Awvo_ready, 1)
                    for s in range(2):
                        act.activation(A[:, :, :].rearrange("p (g a) c -> p g a c", a=2)[:, :, s, :],
                                       SA[:, s, 0:H // 2 * C].rearrange("p (g c) -> p g c", c=C),
                                       ACT.Copy, scale=float(HD) ** -0.5)
                    for j in range(G):
                        ins = act.activation(Wvo[C * j:C * j + C, :, :],
                                             (banks[j % 2])[C * j:C * j + C, :].rearrange("p (t o) -> p t o", o=D), ACT.Copy)
                    ins.then_inc(Awvo_copied, 1)
                    act.wait_ge(stats_step, 1)
                    act.wait_ge(zeroed, 4)
                    act.activation(std[:, :], mv[:, :, 1], ACT.Sqrt, bias=eps_col[:, 0:1]).then_inc(std_done, 1)

                    def copy_xT(b):
                        act.wait_ge(xT_ready, b + 1)
                        act.activation(xnT[:, :], banks[0][:, 0:L], ACT.Copy).then_inc(xT_copied, 1)

                    def split(b, u, before=None):
                        act.wait_ge(prep_ready, b + 1)
                        act.activation(Ls[u][0:KS, :], SA[0:KS, 2, 0:L], ACT.Copy)
                        act.activation(Ln[u][:, :, :].rearrange("p s c -> p (s c)"), SA[:, 2, L:L + QT * C], ACT.Copy).then_inc(hi_done, 1)
                        if before is not None:
                            act.wait_ge(q_stacked[before[1]], 16 * 3 * G * (before[0] + 1))
                        act.activation(q_hi[:, :, :].rearrange("p t q -> p (t q)"), SA[:, 0:2, :].rearrange("p a q -> p (a q)"),
                                       ACT.Copy).then_inc(hi_done, 1)

                    def copy_o(b, t):
                        act.wait_ge(o_ready, NG * b + t + 1)
                        if later(b, 1):
                            act.wait_ge(on_done, b)
                        act.activation(O[:, t, :], banks[int(t in (0, 3))][:, 0:L], ACT.Copy).then_inc(o_copied, 1)

                    def exps(b, t, u):
                        act.wait_ge(scoresT_ready, NG * b + t + 1)
                        if t >= 2 and later(b, 1):
                            act.wait_ge(d_ready, b)
                        if t < 2 and later(b, 2):
                            act.wait_ge(d_ready, b - 1)
                        act.activation(Pr[(NG * u + t) % PR][:, :], SB_[:, :, :].rearrange("p a q -> p (a q)"), ACT.Exp).then_inc(exp_done, 1)

                    copy_xT(0)
                    split(0, 0)
                    copy_xT(1)
                    split(1, 1, (0, 0))

                    def step(i, r, u, more, more2):
                        if more2:
                            copy_xT(i + 2)
                        exps(i, 0, u)
                        exps(i, 1, u)
                        copy_o(i, 0)
                        exps(i, 2, u)
                        copy_o(i, 1)
                        exps(i, 3, u)
                        copy_o(i, 2)
                        copy_o(i, 3)
                        if more2:
                            split(i + 2, (u + 2) % NBUF, turn(r, u, 1))
                    batches(act, step)

                @block.vector
                def _(dve):
                    for u in range(NBUF):
                        ins = dve.memset(Ls[u][KS:P, :].bitcast(F32), 1.0)
                    ins.then_inc(ones_set, 1)
                    for n in range(NT):
                        if n % 16 == 0:
                            dve.wait_ge(x_in[n // 16], 16)
                        ins = dve.bn_stats(stats[:, n, :], X[:, n, :])
                    ins.then_inc(stats2_done, 1)
                    dve.wait_ge(stats2_done, 1)
                    for n in range(NT):
                        ins = dve.bn_aggr(mv[:, n, :], stats[:, n, :])
                    ins.then_inc(stats_step, 1)
                    dve.wait_ge(std_done, 1)
                    dve.reciprocal(rstd[:, :], std[:, :]).then_inc(rstd_done, 1)

                    def normalize(b):
                        if later(b, 1):
                            dve.wait_ge(xT_ready, b)
                        for s in range(QT):
                            n = bass.ds(b * QT + s, 1)
                            ins = dve.tensor_scalar(xn[:, s, :], X[:, n, :].rearrange("p o d -> p (o d)"),
                                                    mv[:, n, 0:1].rearrange("p o d -> p (o d)"), rstd[:, n],
                                                    ALU.subtract, ALU.mult)
                        ins.then_inc(xn_ready, 1)

                    def low_parts(b, u):
                        dve.wait_ge(hi_done, 2 * b + 1)
                        dve.tensor_tensor(Ls[u][2 * C:KS, :], SA[2 * C:KS, 2, 0:L], Ls[u][2 * C:KS, :].bitcast(F32), ALU.subtract)
                        dve.wait_ge(hi_done, 2 * b + 2)
                        dve.tensor_tensor(q_lo[:, :, :].rearrange("p t q -> p (t q)"), SA[:, 0:2, :].rearrange("p a q -> p (a q)"),
                                          q_hi[:, :, :].rearrange("p t q -> p (t q)").bitcast(F32), ALU.subtract).then_inc(lo_done, 1)

                    def maxima(b, t):
                        dve.wait_ge(scores_ready, NG * b + t + 1)
                        if t == 0 and later(b, 1):
                            dve.wait_ge(mT_ready, b)
                        dve.tensor_reduce(nmax[:, G * t:G * t + G, 0], SA[:, 0, :].rearrange("p (j k) -> p j k", k=P),
                                          axis=AX.X, op=ALU.max, negate=True)
                        dve.tensor_reduce(nmax[:, G * t:G * t + G, 1], SA[:, 1:3, :].rearrange("p a (j k) -> p (a j) k", k=L),
                                          axis=AX.X, op=ALU.max, negate=True).then_inc(max_done, 1)

                    def split_max(b, r, u):
                        dve.wait_ge(mT_ready, b + 1)
                        if later(b, 1):
                            rr, uu = turn(r, u, -1)
                            dve.wait_ge(m_stacked[uu], 32 * (rr + 1))
                        dve.tensor_copy(m_hi[:, :], banks[0][0:H * QT, 0:P]).then_inc(mhi_done, 1)
                        dve.wait_ge(mhi_done, b + 1)
                        dve.tensor_tensor(m_lo[:, :], banks[0][0:H * QT, 0:P], m_hi[:, :].bitcast(F32), ALU.subtract).then_inc(m_done, 1)

                    def denominators(b):
                        dve.wait_ge(d_ready, b + 1)
                        dve.reciprocal(rden[:, :], banks[1][:, 0:L]).then_inc(rden_done, 1)
                        dve.wait_ge(rden_done, b + 1)
                        if later(b, 1):
                            dve.wait_ge(on_done, b)
                        dve.sem_inc(shuffles_begun, 1)
                        for t in range(NG):
                            ins = dve.stream_shuffle(rdb[:, t, :], rden[:, :], [C // NG * t] * 32)
                        ins.then_inc(rdb_done, 1)

                    def residual(b):
                        dve.wait_ge(out_ready, b + 1)
                        xb = X[:, bass.ds(b * QT, QT), :]
                        dve.tensor_tensor(xb, banks[1][:, 0:L].rearrange("p (s d) -> p s d", d=D), xb, ALU.add).then_inc(x1_done, 1)

                    dve.wait_ge(rstd_done, 1)
                    normalize(0)
                    normalize(1)
                    low_parts(0, 0)
                    low_parts(1, 1)
                    normalize(2)
                    for t in range(NG):
                        maxima(0, t)
                    split_max(0, 0, 0)

                    def step(i, r, u, more, more2):
                        for t in range(NG):
                            if t == 0 and more2 and later(i, 1):
                                normalize(i + 2)
                            if t == 3 and later(i, 1):
                                residual(i - 1)
                            if more:
                                maxima(i + 1, t)
                            if t == 0 and later(i, 1):
                                denominators(i - 1)
                        if more:
                            split_max(i + 1, *turn(r, u, 1))
                        if more2:
                            low_parts(i + 2, (u + 2) % NBUF)
                    batches(dve, step)
                    denominators(B - 1)
                    residual(B - 1)

                @block.tensor
                def _(pe):
                    pe.wait_ge(consts, 1)
                    pe.wait_ge(wq_in, 16)
                    for g in range(H // 2):
                        pe.transpose(SB_[:, g // 4, g % 4 * D:g % 4 * D + D], wq_sb[:, g * P:g * P + P], ident[:, :])
                    pe.wait_ge(wk_in, 32)
                    for v, w in enumerate((wk_sb, wv_sb)):
                        for g in range(H // 2):
                            at = (v * H // 2 + g) * C
                            ins = pe.transpose(SB_[:, 2, at:at + C], w[:, g * P:g * P + P], ident[0:C, 0:C])
                    ins.then_inc(wT_ready, 1)
                    pe.wait_ge(wT_copied, 2)
                    pe.wait_ge(wo_in, 16)
                    for h in range(H):
                        g, s = h // 2, h % 2
                        rows = slice(HD * s, HD * s + HD)
                        pe.matmul(SA[:, s, g * C:g * C + C], wqT[rows, g, :], wkvT[rows, 0, g, :], start=True, stop=True)
                    for h in range(H):
                        g, s, t, j = h // 2, h % 2, h // G, h % G
                        rows = slice(HD * s, HD * s + HD)
                        ins = pe.matmul(banks[s][C * j:C * j + C, t * D:t * D + D], wkvT[rows, 1, g, :], wo_sb[rows, g, :],
                                        start=True, stop=True)
                    ins.then_inc(Awvo_ready, 1)
                    pe.wait_ge(Awvo_copied, 1)
                    pe.wait_ge(consts, 4)
                    pe.wait_ge(lat_in, 48)
                    pe.wait_ge(ones_set, 1)

                    def transpose_x(b):
                        pe.wait_ge(xn_ready, b + 1)
                        for s in range(QT):
                            ins = pe.transpose(banks[0][:, s * P:s * P + P], xn[:, s, :], ident[:, :])
                        ins.then_inc(xT_ready, 1)

                    def prep(b, u):
                        pe.wait_ge(xT_copied, b + 1)
                        for t in range(NG):
                            pe.matmul(SA[:, t // 2, t % 2 * L:t % 2 * L + L],
                                      A[:, G * t:G * t + G, :].rearrange("p h c -> p (h c)"), xnT[:, :], start=True, stop=True)
                        pe.matmul(SA[0:KS, 2, 0:L], wlat[:, :, :].rearrange("p k c -> p (k c)"), xnT[:, :], start=True, stop=True)
                        for s in range(QT):
                            ins = pe.matmul(SA[:, 2, L + s * C:L + s * C + C], xnT[:, s * P:s * P + P], wlat[:, 0, :],
                                            start=True, stop=True)
                        ins.then_inc(prep_ready, 1)

                    def scores(b, t, u):
                        pe.matmul(SA[:, 0, :], ident_b[:, :], mask[:, :, :].rearrange("p j k -> p (j k)"), start=True, stop=False,
                                  skip_group_check=True)
                        for a_ in range(2):
                            pe.matmul(SA[:, 1 + a_, :].rearrange("p (j k) -> p j k", k=L)[:, :, P:L], ident_b[:, :],
                                      mask[:, 0:2, :], start=True, stop=False, skip_group_check=True)
                        for j in range(G):
                            h = G * t + j
                            pe.matmul(SA[:, 0, j * P:j * P + P], Qs[u][0:KS, h, 0:P], Ls[u][0:KS, 0:P],
                                      start=False, stop=True, skip_group_check=True)
                            ins = pe.matmul(SA[:, 1 + j // 2, j % 2 * L:j % 2 * L + L], Qs[u][0:KS, h, P:L], Ls[u][0:KS, :],
                                            start=False, stop=True, skip_group_check=True)
                        ins.then_inc(scores_ready, 1)

                    def scores_T(b, t, u):
                        K = KS + 2
                        for a_ in range(2):
                            h = G * t + 2 * a_
                            pe.matmul(SB_[:, a_, :], Ls[u][0:K, 0:P], Qs[u][0:K, h:h + 2, :].rearrange("p h q -> p (h q)"),
                                      start=True, stop=True)
                        pe.matmul(SB_[:, 2, :], Ls[u][0:K, P:L], Qs[u][0:K, G * t:G * t + G, P:L],
                                  start=True, stop=True).then_inc(scoresT_ready, 1)

                    def parts(u, t):
                        p = Pr[(4 * u + t) % PR]
                        for j in range(G):
                            yield 0, j, p[:, j * L:j * L + L], slice(0, L)
                        for j in range(G):
                            yield 1, j, p[:, G * L + j * P:G * L + j * P + P], slice(P, L)

                    def weigh(b, t, u, bank):
                        pe.wait_ge(masked, NG * b + t + 1)
                        for s, j, p, q in parts(u, t):
                            ins = pe.matmul(bank[C * j:C * j + C, q], Ln[u][:, s, :], p, start=(s == 0), stop=(s == 1),
                                            skip_group_check=True)
                        ins.then_inc(o_ready, 1)

                    def sums(b, u, bank):
                        for t in range(NG):
                            for s, j, p, q in parts(u, t):
                                ins = pe.matmul(bank[C * j:C * j + C, q], one_t[:, t, :], p, start=(s == 0 and t == 0),
                                                stop=(s == 1 and t == NG - 1), skip_group_check=True)
                        ins.then_inc(d_ready, 1)

                    def project(b, bank):
                        pe.wait_ge(on_done, b + 1)
                        for s in range(QT):
                            for t in range(NG):
                                ins = pe.matmul(bank[:, s * D:s * D + D], On[:, t, s * P:s * P + P], Wvo[:, t, :],
                                                start=(t == 0), stop=(t == NG - 1))
                        ins.then_inc(out_ready, 1)

                    def transpose_max():
                        pe.transpose(banks[0][0:H * QT, 0:P], nmax[:, :, :].rearrange("p h s -> p (h s)"),
                                     ident[:, :]).then_inc(mT_ready, 1)

                    for b in range(2):
                        transpose_x(b)
                        prep(b, b)
                        pe.wait_ge(lo_done, b + 1)
                    pe.wait_ge(q_stacked[0], 16 * 3 * G)
                    for t in range(NG):
                        if t:
                            pe.wait_ge(max_done, t)
                        scores(0, t, 0)
                    pe.wait_ge(max_done, NG)
                    transpose_max()

                    def step(i, r, u, more, more2):
                        r1, u1 = turn(r, u, 1)
                        for t in range(NG):
                            if more:
                                if t == 0:
                                    pe.wait_ge(q_stacked[u1], 16 * 3 * G * (r1 + 1))
                                    pe.wait_ge(lo_done, i + 2)
                                else:
                                    pe.wait_ge(max_done, NG * (i + 1) + t)
                                scores(i + 1, t, u1)
                            if t == 0:
                                pe.wait_ge(m_done, i + 1)
                                if more2:
                                    transpose_x(i + 2)
                                pe.wait_ge(m_stacked[u], 32 * (r + 1))
                            if t > 0 or later(i, 1):
                                pe.wait_ge(exp_done, NG * i + t)
                            scores_T(i, t, u)
                            if t == 1:
                                if later(i, 1):
                                    pe.wait_ge(rden_done, i)
                                weigh(i, 0, u, banks[1])
                            if t == 2:
                                if more2:
                                    pe.wait_ge(xT_copied, i + 3)
                                weigh(i, 1, u, banks[0])
                                if later(i, 1):
                                    pe.wait_ge(o_copied, NG * i + 1)
                                    project(i - 1, banks[1])
                            if t == 3:
                                pe.wait_ge(o_copied, NG * i + 2)
                                weigh(i, 2, u, banks[0])
                        if later(i, 1):
                            pe.wait_ge(x1_done, i)
                        else:
                            pe.wait_ge(o_copied, 1)
                        weigh(i, 3, u, banks[1])
                        if more:
                            pe.wait_ge(max_done, NG * (i + 2))
                            pe.wait_ge(o_copied, NG * i + 3)
                            transpose_max()
                        if more2:
                            prep(i + 2, (u + 2) % NBUF)
                        pe.wait_ge(o_copied, NG * i + 4)
                        sums(i, u, banks[1])
                    batches(pe, step)
                    pe.wait_ge(rden_done, B)
                    project(B - 1, banks[1])

        with ExitStack() as f:
            NH, RU = 4, 2
            w1_hi = sb("w1_hi", [P, E, FH], F32R, f)
            w1_lo = sb("w1_lo", [P, E, FH], F32R, f)
            b1_rows = sb("b1_rows", [HC, P], F32, f)
            b1_col = sb("b1_col", [P, HC], F32, f)
            gw = sb("gw", [E, D], F32, f)
            gw_hi = sb("gw_hi", [P, E], F32R, f)
            gw_lo = sb("gw_lo", [P, E], F32R, f)
            rows = sb("rows", [1, 2, E], F32, f)
            b2_rows = sb("b2_rows", [E, D], F32, f)
            ones = sb("ones", [E, P], F32, f)
            gate_bc = sb("gate_bc", [P, 2, E], F32, f)
            b2_bc = sb("b2_bc", [P, D], F32, f)
            mv2 = [sb(f"mv2_{u}", [P, CT, 2], F32, f) for u in range(2)]
            var_eps = sb("var_eps", [P, CT], F32, f)
            rstd2 = [sb(f"rstd2_{u}", [P, CT], F32, f) for u in range(2)]
            half = sb("half", [P, CT], F32, f)
            euler = sb("euler", [P, CT * E], F32, f)
            xn2 = sb("xn2", [P, CT, D], F32, f)
            x_hi = [sb(f"x_hi{u}", [P, CH], F32R, f) for u in range(2)]
            x_lo = [sb(f"x_lo{u}", [P, CH], F32R, f) for u in range(2)]
            hid = [sb(f"hid{k}", [P, CH], F32, f) for k in range(NH)]
            lg = sb("lg", [P, CT, E], F32, f)
            lg2 = sb("lg2", [P, CT, E], F32, f)
            ms = sb("ms", [P, CT], F32, f)
            rms = sb("rms", [P, CT], F32, f)
            z = sb("z", [P, CT, E], F32, f)
            ez = sb("ez", [P, CT, E], F32, f)
            zmax = sb("zmax", [P, CT], F32, f)
            g = sb("g", [P, CT], F32, f)
            norm = [sb(f"norm{u}", [P, CT], F32, f) for u in range(2)]
            y = [sb(f"y{u}", [P, CT, D], F32, f) for u in range(2)]
            bank_xT, bank_lg = SB_[:, 0, :], SB_[:, 1, :]

            b1_in, b1_done, gw_in, b2_in, f_consts = sem("b1_in"), sem("b1_done"), sem("gw_in"), sem("b2_in"), sem("f_consts")
            gwT_ready, w1h_done, w_done, gwh_done, bc_ready, bc_done = [sem(n_) for n_ in
                ("gwT_ready", "w1h_done", "w_done", "gwh_done", "bc_ready", "bc_done")]
            st2 = sb("st2", [P, CT, 6], F32, f)
            st2_done, aggrs_begun = sem("st2_done"), sem("aggrs_begun")
            fv = sem("fv")
            var_done, rstd2_done, xn2_done, xT2_ready, xhi_done, xlo_done = [sem(n_) for n_ in
                ("var_done", "rstd2_done", "xn2_done", "xT2_ready", "xhi_done", "xlo_done")]
            lg_ready, ms_done, rms_done, z_done, ez_done, norm_done = [sem(n_) for n_ in
                ("lg_ready", "ms_done", "rms_done", "z_done", "ez_done", "norm_done")]
            up_ready, hid_done, down_done, yb_done, y_done = [sem(n_) for n_ in
                ("up_ready", "hid_done", "down_done", "yb_done", "y_done")]
            stored = [sem(f"stored{u}") for u in range(2)]

            def chunks(eng, step):
                for c in range(2):
                    step(c, 0, c, True)
                with eng.Fori(1, NC // 2 - 1) as r:
                    for u in range(2):
                        step(2 * r + u, r, u, True)
                for c in range(NC - 2, NC):
                    step(c, c // 2, c % 2, c + 1 < NC)

            def after(c, k):
                return not isinstance(c, int) or c >= k

            with nc.Block() as block:
                @block.sync
                def _(sp):
                    sp.dma_start(gw[:, :], gate_w).then_inc(gw_in, 16)
                    sp.dma_start(rows[:, 0, :], gate_b.rearrange("(o e) -> o e", o=1)).then_inc(gw_in, 16)
                    sp.dma_start(rows[:, 1, :], rms_w.rearrange("(o e) -> o e", o=1)).then_inc(gw_in, 16)
                    sp.dma_start(b2_rows[:, :], b2).then_inc(b2_in, 16)
                    sp.dma_start(b1_rows[:, :], b1.rearrange("e (a p) -> (e a) p", p=P)).then_inc(b1_in, 16)

                    def step(c, r, u, more):
                        sp.wait_ge(y_done, c + 1)
                        sp.dma_start(out_tiles[:, bass.ds(c * CT, CT), :], y[u][:, :, :]).then_inc(stored[u], 16)
                    chunks(sp, step)
                    for u in range(2):
                        sp.wait_ge(stored[u], 16 * (NC // 2))

                @block.gpsimd
                def _(pool):
                    pool.memset(half[:, :], -0.5)
                    pool.memset(ones[:, :], 1.0)
                    pool.memset(euler[:, :], 2.718281828459045).then_inc(f_consts, 1)
                    pool.wait_ge(f_consts, 1)

                    def rsqrt_var(c, u):
                        pool.wait_ge(var_done, c + 1)
                        pool.tensor_tensor(rstd2[u][:, :], var_eps[:, :], half[:, :], ALU.pow).then_inc(rstd2_done, 1)

                    def gates(c):
                        pool.wait_ge(ms_done, c + 1)
                        pool.tensor_tensor(rms[:, :], ms[:, :], half[:, :], ALU.pow).then_inc(rms_done, 1)
                        pool.wait_ge(z_done, c + 1)
                        pool.tensor_tensor(ez[:, :, :].rearrange("p j e -> p (j e)"), euler[:, :],
                                           z[:, :, :].rearrange("p j e -> p (j e)"), ALU.pow).then_inc(ez_done, 1)

                    rsqrt_var(0, 0)
                    gates(0)

                    def step(c, r, u, more):
                        if more:
                            rsqrt_var(c + 1, 1 - u)
                            gates(c + 1)
                    chunks(pool, step)

                @block.scalar
                def _(act):
                    act.activation(w1_hi[:, :, :], w1_raw[:, :, :], ACT.Copy).then_inc(w1h_done, 1)

                    def high_x(c, u):
                        act.wait_ge(xT2_ready, c + 1)
                        act.activation(x_hi[u][:, :], bank_xT, ACT.Copy).then_inc(xhi_done, 1)

                    high_x(0, 0)
                    act.wait_ge(gwT_ready, 1)
                    act.activation(b1_col[:, :], SB_[:, 1, E * CT:E * CT + HC], ACT.Copy).then_inc(b1_done, 1)
                    act.wait_ge(b1_done, 1)

                    def step(c, r, u, more):
                        for k in range(HC):
                            if more and k == 8:
                                high_x(c + 1, 1 - u)
                            act.wait_ge(up_ready, HC * c + k + 1)
                            if k >= NH or after(c, 1):
                                act.wait_ge(down_done, HC * c + k + 1 - NH)
                            act.activation(hid[k % NH][:, :], SA[:, k % RU, :], ACT.Gelu,
                                           bias=b1_col[:, k:k + 1]).then_inc(hid_done, 1)
                    chunks(act, step)

                @block.vector
                def _(dve):
                    steps = [0]

                    def normalize(c, u):
                        for k in range(CT):
                            n = bass.ds(c * CT + k, 1)
                            ins = dve.bn_stats(st2[:, k, :], X[:, n, :].rearrange("p o d -> p (o d)"))
                        ins.then_inc(st2_done, 1)
                        dve.wait_ge(st2_done, c + 1)
                        dve.sem_inc(aggrs_begun, 1)
                        for k in range(CT):
                            ins = dve.bn_aggr(mv2[u][:, k, :], st2[:, k, :])
                        ins.then_inc(fv, 1)
                        dve.wait_ge(fv, 6 * c + 1)
                        dve.tensor_scalar(var_eps[:, :], mv2[u][:, :, 1], EPS, None, ALU.add).then_inc(var_done, 1)
                        dve.wait_ge(rstd2_done, c + 1)
                        if after(c, 1):
                            dve.wait_ge(xT2_ready, c)
                        for k in range(CT):
                            n = bass.ds(c * CT + k, 1)
                            ins = dve.tensor_scalar(xn2[:, k, :], X[:, n, :].rearrange("p o d -> p (o d)"), mv2[u][:, k, 0:1],
                                                    rstd2[u][:, k:k + 1], ALU.subtract, ALU.mult)
                        ins.then_inc(xn2_done, 1)

                    def low_x(c, u):
                        dve.wait_ge(xhi_done, c + 1)
                        dve.tensor_tensor(x_lo[u][:, :], bank_xT, x_hi[u][:, :].bitcast(F32), ALU.subtract).then_inc(xlo_done, 1)

                    def gate_in(c):
                        dve.wait_ge(lg_ready, c + 1)
                        dve.tensor_tensor(lg[:, :, :], bank_lg[:, 0:CT * E].rearrange("p (j e) -> p j e", e=E),
                                          gate_bc[:, 0:1, :].to_broadcast([P, CT, E]), ALU.add).then_inc(fv, 1)
                        dve.wait_ge(fv, 6 * c + 2)
                        dve.tensor_tensor(lg2[:, :, :], lg[:, :, :], lg[:, :, :], ALU.mult).then_inc(fv, 1)
                        dve.wait_ge(fv, 6 * c + 3)
                        dve.tensor_reduce(g[:, :], lg2[:, :, :], axis=AX.X, op=ALU.add).then_inc(fv, 1)
                        dve.wait_ge(fv, 6 * c + 4)
                        dve.tensor_scalar(ms[:, :], g[:, :], 1.0 / E, 1.1920928955078125e-07, ALU.mult, ALU.add).then_inc(ms_done, 1)

                    def gate_out(c, u):
                        dve.wait_ge(rms_done, c + 1)
                        dve.tensor_tensor(lg2[:, :, :], lg[:, :, :], rms[:, :].unsqueeze(2).to_broadcast([P, CT, E]), ALU.mult).then_inc(fv, 1)
                        dve.wait_ge(fv, 6 * c + 5)
                        dve.tensor_tensor(lg[:, :, :], lg2[:, :, :], gate_bc[:, 1:2, :].to_broadcast([P, CT, E]), ALU.mult).then_inc(fv, 1)
                        dve.wait_ge(fv, 6 * c + 6)
                        dve.tensor_reduce(zmax[:, :], lg[:, :, :], axis=AX.X, op=ALU.max).then_inc(yb_done, 1)
                        dve.wait_ge(yb_done, 8 * c + 1)
                        dve.tensor_tensor(z[:, :, :], lg[:, :, :], zmax[:, :].unsqueeze(2).to_broadcast([P, CT, E]), ALU.subtract).then_inc(z_done, 1)
                        dve.wait_ge(ez_done, c + 1)
                        dve.tensor_reduce(ms[:, :], ez[:, :, :], axis=AX.X, op=ALU.add).then_inc(yb_done, 1)
                        dve.wait_ge(yb_done, 8 * c + 2)
                        dve.reciprocal(g[:, :], ms[:, :]).then_inc(yb_done, 1)
                        dve.wait_ge(yb_done, 8 * c + 3)
                        dve.tensor_scalar(zmax[:, :], g[:, :], 1e-06, None, ALU.add).then_inc(yb_done, 1)
                        dve.wait_ge(yb_done, 8 * c + 4)
                        dve.reciprocal(ms[:, :], zmax[:, :]).then_inc(yb_done, 1)
                        dve.wait_ge(yb_done, 8 * c + 5)
                        dve.tensor_tensor(norm[u][:, :], g[:, :], ms[:, :], ALU.mult).then_inc(norm_done, 1)

                    def finish(c, r, u):
                        dve.wait_ge(down_done, HC * c + HC)
                        if after(c, 2):
                            dve.wait_ge(stored[u], 16 * r)
                        dve.tensor_tensor(y[u][:, :, :], banks[u][:, :].rearrange("p (j d) -> p j d", d=D),
                                          b2_bc[:, :].unsqueeze(1).to_broadcast([P, CT, D]), ALU.add).then_inc(yb_done, 3)
                        dve.wait_ge(norm_done, c + 1)
                        dve.wait_ge(yb_done, 8 * c + 8)
                        for k in range(CT):
                            n = bass.ds(c * CT + k, 1)
                            ins = dve.scalar_tensor_tensor(y[u][:, k, :], y[u][:, k, :], norm[u][:, k:k + 1],
                                                           X[:, n, :].rearrange("p o d -> p (o d)"), ALU.mult, ALU.add)
                        ins.then_inc(y_done, 1)

                    normalize(0, 0)
                    dve.wait_ge(w1h_done, 1)
                    dve.tensor_tensor(w1_lo[:, :, :], w1_raw[:, :, :], w1_hi[:, :, :].bitcast(F32), ALU.subtract)
                    dve.wait_ge(gwT_ready, 1)
                    dve.tensor_copy(gw_hi[:, :], SB_[:, 2, 0:E]).then_inc(gwh_done, 1)
                    dve.wait_ge(gwh_done, 1)
                    dve.tensor_tensor(gw_lo[:, :], SB_[:, 2, 0:E], gw_hi[:, :].bitcast(F32), ALU.subtract)
                    dve.tensor_copy(gate_bc[:, 0, :], SB_[:, 2, E:2 * E])
                    dve.tensor_scalar(gate_bc[:, 1, :], SB_[:, 2, 2 * E:3 * E], 2.0, None, ALU.mult)
                    dve.tensor_copy(b2_bc[:, :], SB_[:, 2, D:2 * D]).then_inc(w_done, 1)
                    low_x(0, 0)
                    dve.wait_ge(w_done, 1)
                    gate_in(0)
                    gate_out(0, 0)

                    def step(c, r, u, more):
                        if more:
                            normalize(c + 1, 1 - u)
                            low_x(c + 1, 1 - u)
                            gate_in(c + 1)
                        finish(c, r, u)
                        if more:
                            gate_out(c + 1, 1 - u)
                    chunks(dve, step)

                @block.tensor
                def _(pe):
                    pe.wait_ge(gw_in, 48)
                    pe.wait_ge(b2_in, 16)
                    pe.wait_ge(f_consts, 1)
                    pe.wait_ge(b1_in, 16)
                    pe.transpose(SB_[:, 1, E * CT:E * CT + HC], b1_rows[:, :], ident[0:HC, 0:HC])
                    pe.transpose(SB_[:, 2, 0:E], gw[:, :], ident[0:E, 0:E])
                    pe.matmul(SB_[:, 2, E:3 * E], ones[0:1, :], rows[:, :, :].rearrange("o a e -> o (a e)"), start=True, stop=True)
                    pe.matmul(SB_[:, 2, D:2 * D], ones[:, :], b2_rows[:, :], start=True, stop=True).then_inc(gwT_ready, 1)

                    def transpose_x(c):
                        pe.wait_ge(xn2_done, c + 1)
                        if after(c, 1):
                            pe.wait_ge(xlo_done, c)
                        for k in range(CT):
                            ins = pe.transpose(bank_xT[:, k * P:k * P + P], xn2[:, k, :], ident[:, :])
                        ins.then_inc(xT2_ready, 1)

                    def logits(c, u):
                        pe.wait_ge(xlo_done, c + 1)
                        if after(c, 1):
                            pe.wait_ge(ms_done, c)
                        for k in range(CT):
                            tok = slice(k * P, k * P + P)
                            for m, (xs, gs) in enumerate(((x_hi, gw_hi), (x_hi, gw_lo), (x_lo, gw_hi))):
                                ins = pe.matmul(bank_lg[:, k * E:k * E + E], xs[u][:, tok], gs[:, :], start=(m == 0), stop=(m == 2))
                        ins.then_inc(lg_ready, 1)

                    def up(c, k, u):
                        if k >= RU or after(c, 1):
                            pe.wait_ge(hid_done, HC * c + k + 1 - RU)
                        unit = slice(k % 2 * P, k % 2 * P + P)
                        for m, (ws, xs) in enumerate(((w1_hi, x_hi), (w1_lo, x_hi), (w1_hi, x_lo))):
                            ins = pe.matmul(SA[:, k % RU, :], ws[:, k // 2, unit], xs[u][:, :], start=(m == 0), stop=(m == 2))
                        ins.then_inc(up_ready, 1)

                    def down(c, k, u):
                        pe.wait_ge(hid_done, HC * c + k + 1)
                        for j in range(CT):
                            ins = pe.matmul(banks[u][:, j * D:j * D + D], hid[k % NH][:, j * P:j * P + P], w2_sb[:, k, :],
                                            start=(k == 0 and j == 0), stop=(k == HC - 1), skip_group_check=True)
                        ins.then_inc(down_done, 1)

                    transpose_x(0)
                    pe.wait_ge(w_done, 1)
                    pe.wait_ge(b1_done, 1)
                    logits(0, 0)

                    def step(c, r, u, more):
                        up(c, 0, u)
                        if after(c, 2):
                            pe.wait_ge(y_done, c - 1)
                        for k in range(1, HC):
                            up(c, k, u)
                            down(c, k - 1, u)
                            if more and k == 6:
                                transpose_x(c + 1)
                            if more and k == 11:
                                logits(c + 1, 1 - u)
                        down(c, HC - 1, u)
                    chunks(pe, step)


_INS = ["L0_attn_x_bld", "L0_attn_Wq", "L0_attn_Wkv_down", "L0_attn_Wk_up", "L0_attn_Wv_up", "L0_attn_Wout", "L0_ffn_gate_w",
        "L0_ffn_gate_b", "L0_ffn_rms_w", "L0_ffn_w1", "L0_ffn_b1", "L0_ffn_w2", "L0_ffn_b2"]


def kernel(**inputs):
    import numpy as _np
    import concourse.bacc as _bacc
    from concourse import mybir as _mybir
    from concourse.bass_utils import run_bass_kernel_spmd as _run

    nc = _bacc.Bacc("TRN2", target_bir_lowering=False, num_devices=1)
    arrays, args = {}, []
    for name in _INS:
        a = _np.ascontiguousarray(inputs[name])
        arrays[f"in_{name}"] = a
        args.append(nc.dram_tensor(f"in_{name}", a.shape, _mybir.dt.from_np(a.dtype), kind="ExternalInput").ap())
    shape = inputs["L0_attn_x_bld"].shape
    args.append(nc.dram_tensor("out_0", shape, _mybir.dt.float32, kind="ExternalOutput").ap())
    preln_block(nc, *args)
    r = _run(nc, [arrays], core_ids=[0])
    return r.results[0]["out_0"]
```

```python
import concourse.bass as bass
from concourse import mybir
from contextlib import ExitStack



def preln_block(nc, x, Wq, Wkv, Wk_up, Wv_up, Wout, gate_w, gate_b, rms_w, w1, b1, w2, b2, out):
    F32, F32R, BF16 = mybir.dt.float32, mybir.dt.float32r, mybir.dt.bfloat16
    ALU, ACT, AX = mybir.AluOpType, mybir.ActivationFunctionType, mybir.AxisListType

    B, L, D = x.shape
    _, H, HD = Wq.shape
    C = Wkv.shape[1]
    E, _, FH = w1.shape
    P = 128
    G = P // C
    NG = H // G
    QT = L // P
    NT = B * QT
    NBUF = 3
    PR = 6
    HC = E * FH // P
    CH = 512
    CT = CH // P
    NC = NT // CT
    EPS = 1e-5
    MASKED = -1.0e30
    KS = 3 * C
    PG = G * L + G * P
    assert QT == 2 and D == P and B % NBUF == 2

    x_tiles = x.rearrange("b (s p) d -> p (b s) d", p=P)
    out_tiles = out.rearrange("b (s p) d -> p (b s) d", p=P)

    keep = ExitStack()
    with keep:
        def sem(name):
            return keep.enter_context(nc.semaphore(name))

        def sb(name, shape, dt=F32, ctx=keep):
            return ctx.enter_context(nc.sbuf_tensor(name, shape, dt))

        X = sb("X", [P, NT, D])
        stats = sb("stats", [P, NT, 6])
        mv = sb("mv", [P, NT, 2])
        std = sb("std", [P, NT])
        rstd = sb("rstd", [P, NT])
        ident = sb("ident", [P, P])
        w1_raw = sb("w1_raw", [P, E, FH])
        w2_sb = sb("w2_sb", [P, HC, D])
        eps_col = sb("eps_col", [P, 1])
        banks = [keep.enter_context(nc.psum_tensor(f"bank{i}", [P, 512], F32)) for i in range(2)]
        SA = keep.enter_context(nc.psum_tensor("scores_q", [P, 3, 512], F32))
        SB_ = keep.enter_context(nc.psum_tensor("scores_k", [P, 3, 512], F32))

        with ExitStack() as a:
            Qs = [sb(f"Qstack{i}", [P, H, L], F32R, a) for i in range(NBUF)]
            Ls = [sb(f"Lstack{i}", [P, L], F32R, a) for i in range(NBUF)]
            Ln = [sb(f"latent{i}", [P, QT, C], F32, a) for i in range(NBUF)]
            Pr = [sb(f"probs{i}", [P, PG], F32, a) for i in range(PR)]
            xn = sb("xn", [P, QT, D], F32, a)
            xnT = sb("xnT", [P, L], F32, a)
            q_hi = sb("q_hi", [P, NG, L], F32R, a)
            q_lo = sb("q_lo", [P, NG, L], F32R, a)
            nmax = sb("nmax", [P, H, QT], F32, a)
            m_hi = sb("m_hi", [H * QT, P], F32R, a)
            m_lo = sb("m_lo", [H * QT, P], F32R, a)
            O = sb("O", [P, NG, L], F32, a)
            On = sb("On", [P, NG, L], F32, a)
            rden = sb("rden", [P, L], F32, a)
            rdb = sb("rdb", [P, NG, L], F32, a)
            wq_sb = Pr[0][:, 0:H * HD]
            wk_sb = Pr[1][0:C, 0:H * HD]
            wv_sb = Pr[2][0:C, 0:H * HD]
            wo_sb = Pr[3][:, 0:H * HD].rearrange("p (g o) -> p g o", o=D)
            wqT = Pr[4][:, 0:H * HD].rearrange("p (g d) -> p g d", d=D)
            wkvT = Pr[5][:, 0:H * C].rearrange("p (v g c) -> p v g c", v=2, c=C)
            wlat = sb("wlat", [P, 3, C], F32, a)
            A = sb("A", [P, H, C], F32, a)
            Wvo = sb("Wvo", [P, NG, D], F32, a)
            ident_b = sb("ident_b", [P, P], BF16, a)
            mask = sb("mask", [P, G, P], BF16, a)
            one_t = sb("one_t", [P, NG, C], F32, a)

            x_in = [sem(f"x_in{i}") for i in range(4)]
            wq_in, wk_in, wo_in, lat_in, ffn_in = sem("wq_in"), sem("wk_in"), sem("wo_in"), sem("lat_in"), sem("ffn_in")
            consts, zeroed = sem("consts"), sem("zeroed")
            masks_set, ones_set, selects_begun, shuffles_begun = sem("masks_set"), sem("ones_set"), sem("selects_begun"), sem("shuffles_begun")
            wT_ready, wT_copied, Awvo_ready, Awvo_copied = sem("wT_ready"), sem("wT_copied"), sem("Awvo_ready"), sem("Awvo_copied")
            stats_step, std_done, rstd_done = sem("stats_step"), sem("std_done"), sem("rstd_done")
            xn_ready, xT_ready, xT_copied = sem("xn_ready"), sem("xT_ready"), sem("xT_copied")
            lat_ready, lat_hi_done, lat_lo_done = sem("lat_ready"), sem("lat_hi_done"), sem("lat_lo_done")
            q_ready, q_hi_done, q_lo_done = sem("q_ready"), sem("q_hi_done"), sem("q_lo_done")
            q_stacked = [sem(f"q_stacked{i}") for i in range(NBUF)]
            m_stacked = [sem(f"m_stacked{i}") for i in range(NBUF)]
            scores_ready, max_done = sem("scores_ready"), sem("max_done")
            mT_ready, mhi_done, m_done = sem("mT_ready"), sem("mhi_done"), sem("m_done")
            scoresT_ready, exp_done, masked = sem("scoresT_ready"), sem("exp_done"), sem("masked")
            o_ready, o_copied, d_ready, rden_done, rdb_done = sem("o_ready"), sem("o_copied"), sem("d_ready"), sem("rden_done"), sem("rdb_done")
            on_done, out_ready, x1_done, stats2_done = sem("on_done"), sem("out_ready"), sem("x1_done"), sem("stats2_done")

            def batches(eng, step):
                for u in range(NBUF):
                    step(u, 0, u, 3)
                with eng.Fori(1, B // NBUF - 1) as r:
                    for u in range(NBUF):
                        step(r * NBUF + u, r, u, 3)
                for i in range(B - 2 - NBUF, B):
                    step(i, i // NBUF, i % NBUF, min(3, B - 1 - i))

            def later(b, k):
                return not isinstance(b, int) or b >= k

            def turn(r, u, k):
                return r + (u + k) // NBUF, (u + k) % NBUF

            with nc.Block() as block:
                @block.sync
                def _(sp):
                    sp.dma_start(wq_sb, Wq.rearrange("d h k -> d (h k)")).then_inc(wq_in, 16)
                    sp.dma_start(wk_sb, Wk_up.rearrange("c h k -> c (h k)")).then_inc(wk_in, 16)
                    sp.dma_start(wv_sb, Wv_up.rearrange("c h k -> c (h k)")).then_inc(wk_in, 16)
                    sp.dma_start(X[:, 0:16, :], x_tiles[:, 0:16, :]).then_inc(x_in[0], 16)
                    sp.dma_start(wo_sb, Wout.rearrange("(g a) k o -> (a k) g o", a=2)).then_inc(wo_in, 16)
                    for n in range(1, 4):
                        sp.dma_start(X[:, 16 * n:16 * n + 16, :], x_tiles[:, 16 * n:16 * n + 16, :]).then_inc(x_in[n], 16)
                    sp.dma_start(w1_raw[:, :, :], w1.rearrange("e d f -> d e f")).then_inc(ffn_in, 16)
                    sp.dma_start(w2_sb[:, :, :], w2.rearrange("e (a p) d -> p (e a) d", p=P)).then_inc(ffn_in, 16)

                    def stack_q(b, r, u):
                        sp.wait_ge(q_lo_done, 2 * b + 2)
                        for j in range(G):
                            for k, src in enumerate((q_hi, q_lo, q_hi)):
                                sp.dma_start(Qs[u][k * C:(k + 1) * C, j::G, :].bitcast(F32),
                                             src[j * C:(j + 1) * C, :, :].bitcast(F32)).then_inc(q_stacked[u], 16)

                    def stack_m(b, r, u):
                        sp.wait_ge(m_done, b + 1)
                        for k, src in enumerate((m_hi, m_lo)):
                            sp.dma_start(Qs[u][KS + k:KS + k + 1, :, :].rearrange("o h (s q) -> o (h s) q", q=P).bitcast(F32),
                                         src[:, :].bitcast(F32)).then_inc(m_stacked[u], 16)

                    stack_q(0, 0, 0)
                    stack_q(1, 0, 1)
                    stack_m(0, 0, 0)

                    def step(i, r, u, ahead):
                        if ahead >= 2:
                            stack_q(i + 2, *turn(r, u, 2))
                        if ahead:
                            stack_m(i + 1, *turn(r, u, 1))
                    batches(sp, step)
                    sp.wait_ge(ffn_in, 32)

                @block.gpsimd
                def _(pool):
                    pool.memset(ident[:, :], 0.0).then_inc(zeroed, 1)
                    pool.memset(mask[:, :, :], 0.0).then_inc(zeroed, 1)
                    pool.memset(one_t[:, :, :], 1.0).then_inc(zeroed, 1)
                    pool.memset(eps_col[:, :], EPS).then_inc(zeroed, 1)
                    pool.wait_ge(zeroed, 4)
                    pool.affine_select(out=ident[:, :], in_=ident[:, :], compare_op=ALU.not_equal, fill=1.0, base=0,
                                       pattern=[[-1, P]], channel_multiplier=1).then_inc(consts, 1)
                    pool.affine_select(out=mask[:, :, :], in_=mask[:, :, :], compare_op=ALU.is_ge, fill=MASKED, base=0,
                                       pattern=[[0, G], [-1, P]], channel_multiplier=1).then_inc(consts, 1)
                    W = C // NG
                    pool.affine_select(out=one_t[:, :, :], in_=one_t[:, :, :], compare_op=ALU.is_ge, fill=0.0, base=0,
                                       pattern=[[-W, NG], [1, C]], channel_multiplier=0).then_inc(masks_set, 1)
                    pool.wait_ge(masks_set, 1)
                    pool.affine_select(out=one_t[:, :, :], in_=one_t[:, :, :], compare_op=ALU.is_ge, fill=0.0, base=W - 1,
                                       pattern=[[W, NG], [-1, C]], channel_multiplier=0).then_inc(consts, 1)
                    pool.wait_ge(consts, 3)
                    pool.tensor_copy(ident_b[:, :], ident[:, :]).then_inc(consts, 1)

                    def mask_probs(b, t, r, u):
                        g = (4 * u + t) % PR
                        pool.wait_ge(exp_done, NG * b + t + 1)
                        pool.sem_inc(selects_begun, 1)
                        low = Pr[g][:, 0:G * L].rearrange("p (j q) -> p j q", q=L)[:, :, 0:P]
                        high = Pr[g][:, G * L:PG].rearrange("p (j q) -> p j q", q=P)
                        for part in (low, high):
                            ins = pool.affine_select(out=part, in_=part, compare_op=ALU.is_ge, fill=0.0, base=0,
                                                     pattern=[[0, G], [1, P]], channel_multiplier=-1)
                        ins.then_inc(masked, 1)

                    def divide(b):
                        pool.wait_ge(o_copied, NG * b + NG)
                        pool.wait_ge(rdb_done, b + 1)
                        if later(b, 1):
                            pool.wait_ge(out_ready, b)
                        pool.tensor_tensor(On[:, :, :], O[:, :, :], rdb[:, :, :], ALU.mult).then_inc(on_done, 1)

                    def step(i, r, u, ahead):
                        for t in range(NG):
                            mask_probs(i, t, r, u)
                            if t == 1 and later(i, 1):
                                divide(i - 1)
                    batches(pool, step)
                    divide(B - 1)

                @block.scalar
                def _(act):
                    act.dma_start(wlat[:, 0, :], Wkv).then_inc(lat_in, 16)
                    act.dma_start(wlat[:, 1, :], Wkv).then_inc(lat_in, 16)
                    act.dma_start(wlat[:, 2, :], Wkv).then_inc(lat_in, 16)
                    act.wait_ge(wT_ready, 1)
                    act.activation(wqT, SB_[:, 0:2, :].rearrange("p a (g d) -> p (a g) d", d=D), ACT.Copy).then_inc(wT_copied, 1)
                    act.activation(wkvT, SB_[:, 2, :].rearrange("p (v g c) -> p v g c", v=2, c=C), ACT.Copy).then_inc(wT_copied, 1)
                    act.wait_ge(Awvo_ready, 1)
                    for s in range(2):
                        act.activation(A[:, :, :].rearrange("p (g a) c -> p g a c", a=2)[:, :, s, :],
                                       SA[:, s, 0:H // 2 * C].rearrange("p (g c) -> p g c", c=C),
                                       ACT.Copy, scale=float(HD) ** -0.5)
                    for j in range(G):
                        ins = act.activation(Wvo[C * j:C * j + C, :, :],
                                             (banks[j % 2])[C * j:C * j + C, :].rearrange("p (t o) -> p t o", o=D), ACT.Copy)
                    ins.then_inc(Awvo_copied, 1)
                    act.wait_ge(stats_step, 1)
                    act.wait_ge(zeroed, 4)
                    act.activation(std[:, :], mv[:, :, 1], ACT.Sqrt, bias=eps_col[:, 0:1]).then_inc(std_done, 1)

                    def copy_xT(b):
                        act.wait_ge(xT_ready, b + 1)
                        act.activation(xnT[:, :], banks[0][:, 0:L], ACT.Copy).then_inc(xT_copied, 1)

                    def high_latents(b, u):
                        act.wait_ge(lat_ready, b + 1)
                        act.activation(Ls[u][0:KS, :], banks[0][0:KS, 0:L], ACT.Copy)
                        act.activation(Ln[u][:, :, :].rearrange("p s c -> p (s c)"), banks[0][:, L:L + QT * C],
                                       ACT.Copy).then_inc(lat_hi_done, 1)

                    def high_queries(b, before):
                        if before is not None:
                            act.wait_ge(q_stacked[before[1]], 16 * 3 * G * (before[0] + 1))
                        for k in range(2):
                            act.wait_ge(q_ready, 2 * b + k + 1)
                            act.activation(q_hi[:, 2 * k:2 * k + 2, :].rearrange("p t q -> p (t q)"), banks[1 - k][:, :],
                                           ACT.Copy).then_inc(q_hi_done, 1)

                    def copy_o(b, t):
                        act.wait_ge(o_ready, NG * b + t + 1)
                        if later(b, 1):
                            act.wait_ge(on_done, b)
                        act.activation(O[:, t, :], banks[int(t != 1)][:, 0:L], ACT.Copy).then_inc(o_copied, 1)

                    def exps(b, t, u):
                        act.wait_ge(scoresT_ready, NG * b + t + 1)
                        if t >= 2 and later(b, 1):
                            act.wait_ge(d_ready, b)
                        if t < 2 and later(b, 2):
                            act.wait_ge(d_ready, b - 1)
                        act.activation(Pr[(NG * u + t) % PR][:, :], SB_[:, :, :].rearrange("p a q -> p (a q)"), ACT.Exp).then_inc(exp_done, 1)

                    copy_xT(0)
                    high_latents(0, 0)
                    high_queries(0, None)
                    copy_xT(1)
                    high_latents(1, 1)
                    high_queries(1, (0, 0))

                    def step(i, r, u, ahead):
                        if ahead >= 2:
                            copy_xT(i + 2)
                        exps(i, 0, u)
                        if ahead >= 2:
                            high_latents(i + 2, (u + 2) % NBUF)
                        exps(i, 1, u)
                        if ahead >= 2:
                            high_queries(i + 2, turn(r, u, 1))
                        exps(i, 2, u)
                        copy_o(i, 0)
                        copy_o(i, 1)
                        exps(i, 3, u)
                        copy_o(i, 2)
                        copy_o(i, 3)
                    batches(act, step)

                @block.vector
                def _(dve):
                    for u in range(NBUF):
                        ins = dve.memset(Ls[u][KS:P, :].bitcast(F32), 1.0)
                    ins.then_inc(ones_set, 1)
                    for n in range(NT):
                        if n % 16 == 0:
                            dve.wait_ge(x_in[n // 16], 16)
                        ins = dve.bn_stats(stats[:, n, :], X[:, n, :])
                    ins.then_inc(stats2_done, 1)
                    dve.wait_ge(stats2_done, 1)
                    for n in range(NT):
                        ins = dve.bn_aggr(mv[:, n, :], stats[:, n, :])
                    ins.then_inc(stats_step, 1)
                    dve.wait_ge(std_done, 1)
                    dve.reciprocal(rstd[:, :], std[:, :]).then_inc(rstd_done, 1)

                    def normalize(b):
                        if later(b, 1):
                            dve.wait_ge(xT_ready, b)
                        for s in range(QT):
                            n = bass.ds(b * QT + s, 1)
                            ins = dve.tensor_scalar(xn[:, s, :], X[:, n, :].rearrange("p o d -> p (o d)"),
                                                    mv[:, n, 0:1].rearrange("p o d -> p (o d)"), rstd[:, n],
                                                    ALU.subtract, ALU.mult)
                        ins.then_inc(xn_ready, 1)

                    def low_latents(b, u):
                        dve.wait_ge(lat_hi_done, b + 1)
                        dve.tensor_tensor(Ls[u][2 * C:KS, :], banks[0][2 * C:KS, 0:L], Ls[u][2 * C:KS, :].bitcast(F32),
                                          ALU.subtract).then_inc(lat_lo_done, 1)

                    def low_queries(b):
                        for k in range(2):
                            dve.wait_ge(q_hi_done, 2 * b + k + 1)
                            dve.tensor_tensor(q_lo[:, 2 * k:2 * k + 2, :].rearrange("p t q -> p (t q)"), banks[1 - k][:, :],
                                              q_hi[:, 2 * k:2 * k + 2, :].rearrange("p t q -> p (t q)").bitcast(F32),
                                              ALU.subtract).then_inc(q_lo_done, 1)

                    def maxima(b, t):
                        dve.wait_ge(scores_ready, NG * b + t + 1)
                        if t == 0 and later(b, 1):
                            dve.wait_ge(mT_ready, b)
                        dve.tensor_reduce(nmax[:, G * t:G * t + G, 0], SA[:, 0, :].rearrange("p (j k) -> p j k", k=P),
                                          axis=AX.X, op=ALU.max, negate=True)
                        dve.tensor_reduce(nmax[:, G * t:G * t + G, 1], SA[:, 1:3, :].rearrange("p a (j k) -> p (a j) k", k=L),
                                          axis=AX.X, op=ALU.max, negate=True).then_inc(max_done, 1)

                    def split_max(b, r, u):
                        dve.wait_ge(mT_ready, b + 1)
                        if later(b, 1):
                            rr, uu = turn(r, u, -1)
                            dve.wait_ge(m_stacked[uu], 32 * (rr + 1))
                        dve.tensor_copy(m_hi[:, :], banks[1][0:H * QT, 0:P]).then_inc(mhi_done, 1)
                        dve.wait_ge(mhi_done, b + 1)
                        dve.tensor_tensor(m_lo[:, :], banks[1][0:H * QT, 0:P], m_hi[:, :].bitcast(F32), ALU.subtract).then_inc(m_done, 1)

                    def invert_sums(b):
                        dve.wait_ge(d_ready, b + 1)
                        if later(b, 1):
                            dve.wait_ge(rdb_done, b)
                        dve.reciprocal(rden[:, :], banks[0][:, 0:L]).then_inc(rden_done, 1)

                    def spread_sums(b):
                        dve.wait_ge(rden_done, b + 1)
                        if later(b, 1):
                            dve.wait_ge(on_done, b)
                        dve.sem_inc(shuffles_begun, 1)
                        for t in range(NG):
                            ins = dve.stream_shuffle(rdb[:, t, :], rden[:, :], [C // NG * t] * 32)
                        ins.then_inc(rdb_done, 1)

                    def residual(b):
                        dve.wait_ge(out_ready, b + 1)
                        xb = X[:, bass.ds(b * QT, QT), :]
                        dve.tensor_tensor(xb, banks[0][:, 0:L].rearrange("p (s d) -> p s d", d=D), xb, ALU.add).then_inc(x1_done, 1)

                    dve.wait_ge(rstd_done, 1)
                    normalize(0)
                    normalize(1)
                    for b in range(2):
                        low_latents(b, b)
                        low_queries(b)
                    normalize(2)
                    for t in range(NG):
                        maxima(0, t)
                    split_max(0, 0, 0)

                    def step(i, r, u, ahead):
                        if later(i, 1):
                            invert_sums(i - 1)
                        for t in range(NG):
                            if ahead:
                                maxima(i + 1, t)
                            if t == 0 and later(i, 1):
                                spread_sums(i - 1)
                            if t == 0 and ahead >= 2:
                                low_latents(i + 2, (u + 2) % NBUF)
                            if t == 1 and ahead >= 2:
                                low_queries(i + 2)
                        if later(i, 1):
                            residual(i - 1)
                        if ahead:
                            split_max(i + 1, *turn(r, u, 1))
                        if ahead >= 3:
                            normalize(i + 3)
                    batches(dve, step)
                    invert_sums(B - 1)
                    spread_sums(B - 1)
                    residual(B - 1)

                @block.tensor
                def _(pe):
                    pe.wait_ge(consts, 1)
                    pe.wait_ge(wq_in, 16)
                    for g in range(H // 2):
                        pe.transpose(SB_[:, g // 4, g % 4 * D:g % 4 * D + D], wq_sb[:, g * P:g * P + P], ident[:, :])
                    pe.wait_ge(wk_in, 32)
                    for v, w in enumerate((wk_sb, wv_sb)):
                        for g in range(H // 2):
                            at = (v * H // 2 + g) * C
                            ins = pe.transpose(SB_[:, 2, at:at + C], w[:, g * P:g * P + P], ident[0:C, 0:C])
                    ins.then_inc(wT_ready, 1)
                    pe.wait_ge(wT_copied, 2)
                    pe.wait_ge(wo_in, 16)
                    for h in range(H):
                        g, s = h // 2, h % 2
                        rows = slice(HD * s, HD * s + HD)
                        pe.matmul(SA[:, s, g * C:g * C + C], wqT[rows, g, :], wkvT[rows, 0, g, :], start=True, stop=True)
                    for h in range(H):
                        g, s, t, j = h // 2, h % 2, h // G, h % G
                        rows = slice(HD * s, HD * s + HD)
                        ins = pe.matmul(banks[s][C * j:C * j + C, t * D:t * D + D], wkvT[rows, 1, g, :], wo_sb[rows, g, :],
                                        start=True, stop=True)
                    ins.then_inc(Awvo_ready, 1)
                    pe.wait_ge(Awvo_copied, 1)
                    pe.wait_ge(consts, 4)
                    pe.wait_ge(lat_in, 48)
                    pe.wait_ge(ones_set, 1)

                    def transpose_x(b):
                        pe.wait_ge(xn_ready, b + 1)
                        for s in range(QT):
                            ins = pe.transpose(banks[0][:, s * P:s * P + P], xn[:, s, :], ident[:, :])
                        ins.then_inc(xT_ready, 1)

                    def latents(b):
                        pe.wait_ge(xT_copied, b + 1)
                        pe.matmul(banks[0][0:KS, 0:L], wlat[:, :, :].rearrange("p k c -> p (k c)"), xnT[:, :], start=True, stop=True)
                        for s in range(QT):
                            ins = pe.matmul(banks[0][:, L + s * C:L + s * C + C], xnT[:, s * P:s * P + P], wlat[:, 0, :],
                                            start=True, stop=True)
                        ins.then_inc(lat_ready, 1)

                    def queries(b, k):
                        for t in range(2 * k, 2 * k + 2):
                            ins = pe.matmul(banks[1 - k][:, t % 2 * L:t % 2 * L + L],
                                            A[:, G * t:G * t + G, :].rearrange("p h c -> p (h c)"), xnT[:, :], start=True, stop=True)
                        ins.then_inc(q_ready, 1)

                    def scores(b, t, u):
                        pe.matmul(SA[:, 0, :], ident_b[:, :], mask[:, :, :].rearrange("p j k -> p (j k)"), start=True, stop=False,
                                  skip_group_check=True)
                        for a_ in range(2):
                            pe.matmul(SA[:, 1 + a_, :].rearrange("p (j k) -> p j k", k=L)[:, :, P:L], ident_b[:, :],
                                      mask[:, 0:2, :], start=True, stop=False, skip_group_check=True)
                        for j in range(G):
                            h = G * t + j
                            pe.matmul(SA[:, 0, j * P:j * P + P], Qs[u][0:KS, h, 0:P], Ls[u][0:KS, 0:P],
                                      start=False, stop=True, skip_group_check=True)
                            ins = pe.matmul(SA[:, 1 + j // 2, j % 2 * L:j % 2 * L + L], Qs[u][0:KS, h, P:L], Ls[u][0:KS, :],
                                            start=False, stop=True, skip_group_check=True)
                        ins.then_inc(scores_ready, 1)

                    def scores_T(b, t, u):
                        K = KS + 2
                        for a_ in range(2):
                            h = G * t + 2 * a_
                            pe.matmul(SB_[:, a_, :], Ls[u][0:K, 0:P], Qs[u][0:K, h:h + 2, :].rearrange("p h q -> p (h q)"),
                                      start=True, stop=True)
                        pe.matmul(SB_[:, 2, :], Ls[u][0:K, P:L], Qs[u][0:K, G * t:G * t + G, P:L],
                                  start=True, stop=True).then_inc(scoresT_ready, 1)

                    def parts(u, t):
                        p = Pr[(4 * u + t) % PR]
                        for j in range(G):
                            yield 0, j, p[:, j * L:j * L + L], slice(0, L)
                        for j in range(G):
                            yield 1, j, p[:, G * L + j * P:G * L + j * P + P], slice(P, L)

                    def weigh(b, t, u, bank):
                        pe.wait_ge(masked, NG * b + t + 1)
                        for s, j, p, q in parts(u, t):
                            ins = pe.matmul(bank[C * j:C * j + C, q], Ln[u][:, s, :], p, start=(s == 0), stop=(s == 1),
                                            skip_group_check=True)
                        ins.then_inc(o_ready, 1)

                    def sums(b, u, bank):
                        for t in range(NG):
                            pe.wait_ge(masked, NG * b + t + 1)
                            for s, j, p, q in parts(u, t):
                                ins = pe.matmul(bank[C * j:C * j + C, q], one_t[:, t, :], p, start=(s == 0 and t == 0),
                                                stop=(s == 1 and t == NG - 1), skip_group_check=True)
                        ins.then_inc(d_ready, 1)

                    def project(b, bank):
                        pe.wait_ge(on_done, b + 1)
                        for s in range(QT):
                            for t in range(NG):
                                ins = pe.matmul(bank[:, s * D:s * D + D], On[:, t, s * P:s * P + P], Wvo[:, t, :],
                                                start=(t == 0), stop=(t == NG - 1))
                        ins.then_inc(out_ready, 1)

                    def transpose_max():
                        pe.transpose(banks[1][0:H * QT, 0:P], nmax[:, :, :].rearrange("p h s -> p (h s)"),
                                     ident[:, :]).then_inc(mT_ready, 1)

                    for b in range(2):
                        if b:
                            pe.wait_ge(q_lo_done, 2)
                        transpose_x(b)
                        latents(b)
                        queries(b, 0)
                        pe.wait_ge(lat_lo_done, b + 1)
                        queries(b, 1)
                    pe.wait_ge(q_stacked[0], 16 * 3 * G)
                    for t in range(NG):
                        if t:
                            pe.wait_ge(max_done, t)
                        scores(0, t, 0)
                    pe.wait_ge(max_done, NG)
                    pe.wait_ge(q_lo_done, 4)
                    transpose_max()

                    def step(i, r, u, ahead):
                        r1, u1 = turn(r, u, 1)
                        for t in range(NG):
                            if ahead:
                                if t == 0:
                                    pe.wait_ge(q_stacked[u1], 16 * 3 * G * (r1 + 1))
                                pe.wait_ge(max_done, NG * (i + 1) + t)
                                scores(i + 1, t, u1)
                            if t == 0:
                                if later(i, 1):
                                    pe.wait_ge(rden_done, i)
                                if ahead >= 2:
                                    transpose_x(i + 2)
                                pe.wait_ge(m_stacked[u], 32 * (r + 1))
                            if t > 0 or later(i, 1):
                                pe.wait_ge(exp_done, NG * i + t)
                            scores_T(i, t, u)
                            if t == 0 and ahead >= 2:
                                latents(i + 2)
                            if t == 1 and ahead >= 2:
                                if later(i, 1):
                                    pe.wait_ge(o_copied, NG * i)
                                else:
                                    pe.wait_ge(m_done, 1)
                                queries(i + 2, 0)
                                pe.wait_ge(lat_lo_done, i + 3)
                                queries(i + 2, 1)
                            if t == 2:
                                if ahead >= 2:
                                    pe.wait_ge(q_lo_done, 2 * i + 5)
                                else:
                                    pe.wait_ge(o_copied, NG * i)
                                weigh(i, 0, u, banks[1])
                                if ahead >= 2:
                                    pe.wait_ge(q_lo_done, 2 * i + 6)
                                weigh(i, 1, u, banks[0])
                            if t == 3:
                                pe.wait_ge(o_copied, NG * i + 1)
                                weigh(i, 2, u, banks[1])
                                pe.wait_ge(o_copied, NG * i + 2)
                                if later(i, 1):
                                    project(i - 1, banks[0])
                        pe.wait_ge(o_copied, NG * i + 3)
                        if ahead:
                            pe.wait_ge(max_done, NG * (i + 2))
                            transpose_max()
                        if later(i, 1):
                            pe.wait_ge(x1_done, i)
                        sums(i, u, banks[0])
                        if ahead:
                            pe.wait_ge(m_done, i + 2)
                        weigh(i, 3, u, banks[1])
                    batches(pe, step)
                    pe.wait_ge(rden_done, B)
                    project(B - 1, banks[0])

        with ExitStack() as f:
            NH, RU = 4, 2
            w1_hi = sb("w1_hi", [P, E, FH], F32R, f)
            w1_lo = sb("w1_lo", [P, E, FH], F32R, f)
            b1_rows = sb("b1_rows", [HC, P], F32, f)
            b1_col = sb("b1_col", [P, HC], F32, f)
            gw = sb("gw", [E, D], F32, f)
            gw_hi = sb("gw_hi", [P, E], F32R, f)
            gw_lo = sb("gw_lo", [P, E], F32R, f)
            rows = sb("rows", [1, 2, E], F32, f)
            b2_rows = sb("b2_rows", [E, D], F32, f)
            ones = sb("ones", [E, P], F32, f)
            gate_bc = sb("gate_bc", [P, 2, E], F32, f)
            b2_bc = sb("b2_bc", [P, D], F32, f)
            mv2 = [sb(f"mv2_{u}", [P, CT, 2], F32, f) for u in range(2)]
            var_eps = sb("var_eps", [P, CT], F32, f)
            rstd2 = [sb(f"rstd2_{u}", [P, CT], F32, f) for u in range(2)]
            half = sb("half", [P, CT], F32, f)
            euler = sb("euler", [P, CT * E], F32, f)
            xn2 = sb("xn2", [P, CT, D], F32, f)
            x_hi = [sb(f"x_hi{u}", [P, CH], F32R, f) for u in range(2)]
            x_lo = [sb(f"x_lo{u}", [P, CH], F32R, f) for u in range(2)]
            hid = [sb(f"hid{k}", [P, CH], F32, f) for k in range(NH)]
            lg = sb("lg", [P, CT, E], F32, f)
            lg2 = sb("lg2", [P, CT, E], F32, f)
            ms = sb("ms", [P, CT], F32, f)
            rms = sb("rms", [P, CT], F32, f)
            z = sb("z", [P, CT, E], F32, f)
            ez = sb("ez", [P, CT, E], F32, f)
            zmax = sb("zmax", [P, CT], F32, f)
            g = sb("g", [P, CT], F32, f)
            norm = [sb(f"norm{u}", [P, CT], F32, f) for u in range(2)]
            y = [sb(f"y{u}", [P, CT, D], F32, f) for u in range(2)]
            bank_xT, bank_lg = SB_[:, 0, :], SB_[:, 1, :]

            b1_in, b1_done, gw_in, b2_in, f_consts = sem("b1_in"), sem("b1_done"), sem("gw_in"), sem("b2_in"), sem("f_consts")
            gwT_ready, w1h_done, w_done, gwh_done, bc_ready, bc_done = [sem(n_) for n_ in
                ("gwT_ready", "w1h_done", "w_done", "gwh_done", "bc_ready", "bc_done")]
            st2 = sb("st2", [P, CT, 6], F32, f)
            st2_done, aggrs_begun = sem("st2_done"), sem("aggrs_begun")
            fv = sem("fv")
            var_done, rstd2_done, xn2_done, xT2_ready, xhi_done, xlo_done = [sem(n_) for n_ in
                ("var_done", "rstd2_done", "xn2_done", "xT2_ready", "xhi_done", "xlo_done")]
            lg_ready, ms_done, rms_done, z_done, ez_done, norm_done = [sem(n_) for n_ in
                ("lg_ready", "ms_done", "rms_done", "z_done", "ez_done", "norm_done")]
            up_ready, hid_done, down_done, yb_done, y_done = [sem(n_) for n_ in
                ("up_ready", "hid_done", "down_done", "yb_done", "y_done")]
            stored = [sem(f"stored{u}") for u in range(2)]

            def chunks(eng, step):
                for c in range(2):
                    step(c, 0, c, True)
                with eng.Fori(1, NC // 2 - 1) as r:
                    for u in range(2):
                        step(2 * r + u, r, u, True)
                for c in range(NC - 2, NC):
                    step(c, c // 2, c % 2, c + 1 < NC)

            def after(c, k):
                return not isinstance(c, int) or c >= k

            with nc.Block() as block:
                @block.sync
                def _(sp):
                    sp.dma_start(gw[:, :], gate_w).then_inc(gw_in, 16)
                    sp.dma_start(rows[:, 0, :], gate_b.rearrange("(o e) -> o e", o=1)).then_inc(gw_in, 16)
                    sp.dma_start(rows[:, 1, :], rms_w.rearrange("(o e) -> o e", o=1)).then_inc(gw_in, 16)
                    sp.dma_start(b2_rows[:, :], b2).then_inc(b2_in, 16)
                    sp.dma_start(b1_rows[:, :], b1.rearrange("e (a p) -> (e a) p", p=P)).then_inc(b1_in, 16)

                    def step(c, r, u, more):
                        sp.wait_ge(y_done, c + 1)
                        sp.dma_start(out_tiles[:, bass.ds(c * CT, CT), :], y[u][:, :, :]).then_inc(stored[u], 16)
                    chunks(sp, step)
                    for u in range(2):
                        sp.wait_ge(stored[u], 16 * (NC // 2))

                @block.gpsimd
                def _(pool):
                    pool.memset(half[:, :], -0.5)
                    pool.memset(ones[:, :], 1.0)
                    pool.memset(euler[:, :], 2.718281828459045).then_inc(f_consts, 1)
                    pool.wait_ge(f_consts, 1)

                    def rsqrt_var(c, u):
                        pool.wait_ge(var_done, c + 1)
                        pool.tensor_tensor(rstd2[u][:, :], var_eps[:, :], half[:, :], ALU.pow).then_inc(rstd2_done, 1)

                    def gates(c):
                        pool.wait_ge(ms_done, c + 1)
                        pool.tensor_tensor(rms[:, :], ms[:, :], half[:, :], ALU.pow).then_inc(rms_done, 1)
                        pool.wait_ge(z_done, c + 1)
                        pool.tensor_tensor(ez[:, :, :].rearrange("p j e -> p (j e)"), euler[:, :],
                                           z[:, :, :].rearrange("p j e -> p (j e)"), ALU.pow).then_inc(ez_done, 1)

                    rsqrt_var(0, 0)
                    gates(0)

                    def step(c, r, u, more):
                        if more:
                            rsqrt_var(c + 1, 1 - u)
                            gates(c + 1)
                    chunks(pool, step)

                @block.scalar
                def _(act):
                    act.activation(w1_hi[:, :, :], w1_raw[:, :, :], ACT.Copy).then_inc(w1h_done, 1)

                    def high_x(c, u):
                        act.wait_ge(xT2_ready, c + 1)
                        act.activation(x_hi[u][:, :], bank_xT, ACT.Copy).then_inc(xhi_done, 1)

                    high_x(0, 0)
                    act.wait_ge(gwT_ready, 1)
                    act.activation(b1_col[:, :], SB_[:, 1, E * CT:E * CT + HC], ACT.Copy).then_inc(b1_done, 1)
                    act.wait_ge(b1_done, 1)

                    def step(c, r, u, more):
                        for k in range(HC):
                            if more and k == 8:
                                high_x(c + 1, 1 - u)
                            act.wait_ge(up_ready, HC * c + k + 1)
                            if k >= NH or after(c, 1):
                                act.wait_ge(down_done, HC * c + k + 1 - NH)
                            act.activation(hid[k % NH][:, :], SA[:, k % RU, :], ACT.Gelu,
                                           bias=b1_col[:, k:k + 1]).then_inc(hid_done, 1)
                    chunks(act, step)

                @block.vector
                def _(dve):
                    steps = [0]

                    def normalize(c, u):
                        for k in range(CT):
                            n = bass.ds(c * CT + k, 1)
                            ins = dve.bn_stats(st2[:, k, :], X[:, n, :].rearrange("p o d -> p (o d)"))
                        ins.then_inc(st2_done, 1)
                        dve.wait_ge(st2_done, c + 1)
                        dve.sem_inc(aggrs_begun, 1)
                        for k in range(CT):
                            ins = dve.bn_aggr(mv2[u][:, k, :], st2[:, k, :])
                        ins.then_inc(fv, 1)
                        dve.wait_ge(fv, 6 * c + 1)
                        dve.tensor_scalar(var_eps[:, :], mv2[u][:, :, 1], EPS, None, ALU.add).then_inc(var_done, 1)
                        dve.wait_ge(rstd2_done, c + 1)
                        if after(c, 1):
                            dve.wait_ge(xT2_ready, c)
                        for k in range(CT):
                            n = bass.ds(c * CT + k, 1)
                            ins = dve.tensor_scalar(xn2[:, k, :], X[:, n, :].rearrange("p o d -> p (o d)"), mv2[u][:, k, 0:1],
                                                    rstd2[u][:, k:k + 1], ALU.subtract, ALU.mult)
                        ins.then_inc(xn2_done, 1)

                    def low_x(c, u):
                        dve.wait_ge(xhi_done, c + 1)
                        dve.tensor_tensor(x_lo[u][:, :], bank_xT, x_hi[u][:, :].bitcast(F32), ALU.subtract).then_inc(xlo_done, 1)

                    def gate_in(c):
                        dve.wait_ge(lg_ready, c + 1)
                        dve.tensor_tensor(lg[:, :, :], bank_lg[:, 0:CT * E].rearrange("p (j e) -> p j e", e=E),
                                          gate_bc[:, 0:1, :].to_broadcast([P, CT, E]), ALU.add).then_inc(fv, 1)
                        dve.wait_ge(fv, 6 * c + 2)
                        dve.tensor_tensor(lg2[:, :, :], lg[:, :, :], lg[:, :, :], ALU.mult).then_inc(fv, 1)
                        dve.wait_ge(fv, 6 * c + 3)
                        dve.tensor_reduce(g[:, :], lg2[:, :, :], axis=AX.X, op=ALU.add).then_inc(fv, 1)
                        dve.wait_ge(fv, 6 * c + 4)
                        dve.tensor_scalar(ms[:, :], g[:, :], 1.0 / E, 1.1920928955078125e-07, ALU.mult, ALU.add).then_inc(ms_done, 1)

                    def gate_out(c, u):
                        dve.wait_ge(rms_done, c + 1)
                        dve.tensor_tensor(lg2[:, :, :], lg[:, :, :], rms[:, :].unsqueeze(2).to_broadcast([P, CT, E]), ALU.mult).then_inc(fv, 1)
                        dve.wait_ge(fv, 6 * c + 5)
                        dve.tensor_tensor(lg[:, :, :], lg2[:, :, :], gate_bc[:, 1:2, :].to_broadcast([P, CT, E]), ALU.mult).then_inc(fv, 1)
                        dve.wait_ge(fv, 6 * c + 6)
                        dve.tensor_reduce(zmax[:, :], lg[:, :, :], axis=AX.X, op=ALU.max).then_inc(yb_done, 1)
                        dve.wait_ge(yb_done, 8 * c + 1)
                        dve.tensor_tensor(z[:, :, :], lg[:, :, :], zmax[:, :].unsqueeze(2).to_broadcast([P, CT, E]), ALU.subtract).then_inc(z_done, 1)
                        dve.wait_ge(ez_done, c + 1)
                        dve.tensor_reduce(ms[:, :], ez[:, :, :], axis=AX.X, op=ALU.add).then_inc(yb_done, 1)
                        dve.wait_ge(yb_done, 8 * c + 2)
                        dve.reciprocal(g[:, :], ms[:, :]).then_inc(yb_done, 1)
                        dve.wait_ge(yb_done, 8 * c + 3)
                        dve.tensor_scalar(zmax[:, :], g[:, :], 1e-06, None, ALU.add).then_inc(yb_done, 1)
                        dve.wait_ge(yb_done, 8 * c + 4)
                        dve.reciprocal(ms[:, :], zmax[:, :]).then_inc(yb_done, 1)
                        dve.wait_ge(yb_done, 8 * c + 5)
                        dve.tensor_tensor(norm[u][:, :], g[:, :], ms[:, :], ALU.mult).then_inc(norm_done, 1)

                    def finish(c, r, u):
                        dve.wait_ge(down_done, HC * c + HC)
                        if after(c, 2):
                            dve.wait_ge(stored[u], 16 * r)
                        dve.tensor_tensor(y[u][:, :, :], banks[u][:, :].rearrange("p (j d) -> p j d", d=D),
                                          b2_bc[:, :].unsqueeze(1).to_broadcast([P, CT, D]), ALU.add).then_inc(yb_done, 3)
                        dve.wait_ge(norm_done, c + 1)
                        dve.wait_ge(yb_done, 8 * c + 8)
                        for k in range(CT):
                            n = bass.ds(c * CT + k, 1)
                            ins = dve.scalar_tensor_tensor(y[u][:, k, :], y[u][:, k, :], norm[u][:, k:k + 1],
                                                           X[:, n, :].rearrange("p o d -> p (o d)"), ALU.mult, ALU.add)
                        ins.then_inc(y_done, 1)

                    normalize(0, 0)
                    dve.wait_ge(w1h_done, 1)
                    dve.tensor_tensor(w1_lo[:, :, :], w1_raw[:, :, :], w1_hi[:, :, :].bitcast(F32), ALU.subtract)
                    dve.wait_ge(gwT_ready, 1)
                    dve.tensor_copy(gw_hi[:, :], SB_[:, 2, 0:E]).then_inc(gwh_done, 1)
                    dve.wait_ge(gwh_done, 1)
                    dve.tensor_tensor(gw_lo[:, :], SB_[:, 2, 0:E], gw_hi[:, :].bitcast(F32), ALU.subtract)
                    dve.tensor_copy(gate_bc[:, 0, :], SB_[:, 2, E:2 * E])
                    dve.tensor_scalar(gate_bc[:, 1, :], SB_[:, 2, 2 * E:3 * E], 2.0, None, ALU.mult)
                    dve.tensor_copy(b2_bc[:, :], SB_[:, 2, D:2 * D]).then_inc(w_done, 1)
                    low_x(0, 0)
                    dve.wait_ge(w_done, 1)
                    gate_in(0)
                    gate_out(0, 0)

                    def step(c, r, u, more):
                        if more:
                            normalize(c + 1, 1 - u)
                            low_x(c + 1, 1 - u)
                            gate_in(c + 1)
                        finish(c, r, u)
                        if more:
                            gate_out(c + 1, 1 - u)
                    chunks(dve, step)

                @block.tensor
                def _(pe):
                    pe.wait_ge(gw_in, 48)
                    pe.wait_ge(b2_in, 16)
                    pe.wait_ge(f_consts, 1)
                    pe.wait_ge(b1_in, 16)
                    pe.transpose(SB_[:, 1, E * CT:E * CT + HC], b1_rows[:, :], ident[0:HC, 0:HC])
                    pe.transpose(SB_[:, 2, 0:E], gw[:, :], ident[0:E, 0:E])
                    pe.matmul(SB_[:, 2, E:3 * E], ones[0:1, :], rows[:, :, :].rearrange("o a e -> o (a e)"), start=True, stop=True)
                    pe.matmul(SB_[:, 2, D:2 * D], ones[:, :], b2_rows[:, :], start=True, stop=True).then_inc(gwT_ready, 1)

                    def transpose_x(c):
                        pe.wait_ge(xn2_done, c + 1)
                        if after(c, 1):
                            pe.wait_ge(xlo_done, c)
                        for k in range(CT):
                            ins = pe.transpose(bank_xT[:, k * P:k * P + P], xn2[:, k, :], ident[:, :])
                        ins.then_inc(xT2_ready, 1)

                    def logits(c, u):
                        pe.wait_ge(xlo_done, c + 1)
                        if after(c, 1):
                            pe.wait_ge(ms_done, c)
                        for k in range(CT):
                            tok = slice(k * P, k * P + P)
                            for m, (xs, gs) in enumerate(((x_hi, gw_hi), (x_hi, gw_lo), (x_lo, gw_hi))):
                                ins = pe.matmul(bank_lg[:, k * E:k * E + E], xs[u][:, tok], gs[:, :], start=(m == 0), stop=(m == 2))
                        ins.then_inc(lg_ready, 1)

                    def up(c, k, u):
                        if k >= RU or after(c, 1):
                            pe.wait_ge(hid_done, HC * c + k + 1 - RU)
                        unit = slice(k % 2 * P, k % 2 * P + P)
                        for m, (ws, xs) in enumerate(((w1_hi, x_hi), (w1_lo, x_hi), (w1_hi, x_lo))):
                            ins = pe.matmul(SA[:, k % RU, :], ws[:, k // 2, unit], xs[u][:, :], start=(m == 0), stop=(m == 2))
                        ins.then_inc(up_ready, 1)

                    def down(c, k, u):
                        pe.wait_ge(hid_done, HC * c + k + 1)
                        for j in range(CT):
                            ins = pe.matmul(banks[u][:, j * D:j * D + D], hid[k % NH][:, j * P:j * P + P], w2_sb[:, k, :],
                                            start=(k == 0 and j == 0), stop=(k == HC - 1), skip_group_check=True)
                        ins.then_inc(down_done, 1)

                    transpose_x(0)
                    pe.wait_ge(w_done, 1)
                    pe.wait_ge(b1_done, 1)
                    logits(0, 0)

                    def step(c, r, u, more):
                        up(c, 0, u)
                        if after(c, 2):
                            pe.wait_ge(y_done, c - 1)
                        for k in range(1, HC):
                            up(c, k, u)
                            down(c, k - 1, u)
                            if more and k == 6:
                                transpose_x(c + 1)
                            if more and k == 11:
                                logits(c + 1, 1 - u)
                        down(c, HC - 1, u)
                    chunks(pe, step)


_INS = ["L0_attn_x_bld", "L0_attn_Wq", "L0_attn_Wkv_down", "L0_attn_Wk_up", "L0_attn_Wv_up", "L0_attn_Wout", "L0_ffn_gate_w",
        "L0_ffn_gate_b", "L0_ffn_rms_w", "L0_ffn_w1", "L0_ffn_b1", "L0_ffn_w2", "L0_ffn_b2"]


def kernel(**inputs):
    import numpy as _np
    import concourse.bacc as _bacc
    from concourse import mybir as _mybir
    from concourse.bass_utils import run_bass_kernel_spmd as _run

    nc = _bacc.Bacc("TRN2", target_bir_lowering=False, num_devices=1)
    arrays, args = {}, []
    for name in _INS:
        a = _np.ascontiguousarray(inputs[name])
        arrays[f"in_{name}"] = a
        args.append(nc.dram_tensor(f"in_{name}", a.shape, _mybir.dt.from_np(a.dtype), kind="ExternalInput").ap())
    shape = inputs["L0_attn_x_bld"].shape
    args.append(nc.dram_tensor("out_0", shape, _mybir.dt.float32, kind="ExternalOutput").ap())
    preln_block(nc, *args)
    r = _run(nc, [arrays], core_ids=[0])
    return r.results[0]["out_0"]
```

```python
import concourse.bass as bass
from concourse import mybir
from contextlib import ExitStack



def preln_block(nc, x, Wq, Wkv, Wk_up, Wv_up, Wout, gate_w, gate_b, rms_w, w1, b1, w2, b2, out):
    F32, F32R = mybir.dt.float32, mybir.dt.float32r
    ALU, ACT, AX = mybir.AluOpType, mybir.ActivationFunctionType, mybir.AxisListType

    B, L, D = x.shape
    _, H, HD = Wq.shape
    C = Wkv.shape[1]
    E, _, FH = w1.shape
    P = 128
    G = P // C
    NG = H // G
    QT = L // P
    NT = B * QT
    NBUF = 3
    PR = 6
    HC = E * FH // P
    CH = 512
    CT = CH // P
    NC = NT // CT
    SQ = NT // 4
    FIRST = SQ // 4
    EPS = 1e-5
    MASKED = -1.0e30
    KS = 3 * C
    PG = G * L + G * P
    assert QT == 2 and D == P and B % NBUF == 2

    x_tiles = x.rearrange("b (s p) d -> p (b s) d", p=P)
    out_tiles = out.rearrange("b (s p) d -> p (b s) d", p=P)

    keep = ExitStack()
    with keep:
        def sem(name):
            return keep.enter_context(nc.semaphore(name))

        def sb(name, shape, dt=F32):
            return keep.enter_context(nc.sbuf_tensor(name, shape, dt))

        X = sb("X", [P, NT, D])
        stats = sb("stats", [P, NT, 6])
        mv = sb("mv", [P, NT, 2])
        std = sb("std", [P, NT])
        rstd = sb("rstd", [P, NT])
        ident = sb("ident", [P, P])
        w1_raw = sb("w1_raw", [P, E, FH])
        w2_raw = sb("w2_raw", [P, HC, D])
        banks = [keep.enter_context(nc.psum_tensor(f"bank{i}", [P, 512], F32)) for i in range(2)]
        SA = keep.enter_context(nc.psum_tensor("scores_q", [P, 3, 512], F32))
        SB_ = keep.enter_context(nc.psum_tensor("scores_k", [P, 3, 512], F32))

        Qs = [sb(f"Qstack{i}", [P, H, L], F32R) for i in range(NBUF)]
        Ls = [sb(f"Lstack{i}", [P, L], F32R) for i in range(NBUF)]
        Ln = [sb(f"latent{i}", [P, QT, C], F32) for i in range(NBUF)]
        Pr = [sb(f"probs{i}", [P, PG + G * P], F32) for i in range(PR)]
        xn = sb("xn", [P, QT, D], F32)
        xnT = sb("xnT", [P, L], F32)
        q = sb("q", [P, NG, L], F32)
        xT_hi = sb("xT_hi", [P, L], F32R)
        xT_lo = sb("xT_lo", [P, L], F32R)
        q_hi = sb("q_hi", [P, NG, L], F32R)
        q_lo = sb("q_lo", [P, NG, L], F32R)
        qmax = sb("qmax", [P, H, QT], F32)
        m_hi = sb("m_hi", [H * QT, P], F32R)
        m_lo = sb("m_lo", [H * QT, P], F32R)
        O = sb("O", [P, NG, L], F32)
        On = sb("On", [P, NG, L], F32)
        rden = sb("rden", [P, L], F32)
        rdb = sb("rdb", [P, NG, L], F32)
        wq_sb = Pr[0][:, 0:H * HD]
        wk_sb = Pr[1][0:C, 0:H * HD]
        wv_sb = Pr[2][0:C, 0:H * HD]
        wo_sb = Pr[3][:, 0:H * HD].rearrange("p (g o) -> p g o", o=D)
        wqT = Pr[4][:, 0:H * HD].rearrange("p (g d) -> p g d", d=D)
        wkT = Pr[5][:, 0:H * C].rearrange("p (g s c) -> p g s c", s=2, c=C)
        wvT = Pr[5][:, H * C:H * C + H // 2 * C].rearrange("p (g c) -> p g c", c=C)
        wlat = sb("wlat", [P, C], F32)
        wlat_hi, wlat_lo = sb("wlat_hi", [P, 3, C], F32R), sb("wlat_lo", [P, 3, C], F32R)
        A_hi, A_lo = sb("A_hi", [P, H, C], F32R), sb("A_lo", [P, H, C], F32R)
        A_full = O[:, 0:H * C // L, :].rearrange("p t q -> p (t q)")
        Wvo = sb("Wvo", [P, NG, D], F32)
        mask = sb("mask", [P, L])
        one_t = sb("one_t", [P, NG, C], F32)
        neg_half = sb("neg_half", [P, SQ], F32)

        x_in = [sem(f"x_in{i}") for i in range(5)]
        wq_in, wk_in, wo_in, lat_in, ffn_in = sem("wq_in"), sem("wk_in"), sem("wo_in"), sem("lat_in"), sem("ffn_in")
        consts, zeroed = sem("consts"), sem("zeroed")
        masks_set, ones_set, selects_begun, shuffles_begun = sem("masks_set"), sem("ones_set"), sem("selects_begun"), sem("shuffles_begun")
        k_zeroed, wT_ready, wT_copied, v_copied = sem("k_zeroed"), sem("wT_ready"), sem("wT_copied"), sem("v_copied")
        A_ready, A_copied, vo_ready, vo_copied = sem("A_ready"), sem("A_copied"), sem("vo_ready"), sem("vo_copied")
        var_ready, rstd_done = sem("var_ready"), sem("rstd_done")
        maxima_begun = sem("maxima_begun")
        stats_done, aggr_done = sem("stats_done"), sem("aggr_done")
        xn_ready, xT_ready, xT_copied, xT_lo_done = sem("xn_ready"), sem("xT_ready"), sem("xT_copied"), sem("xT_lo_done")
        wlat_hi_done, wlat_done, A_lo_done = sem("wlat_hi_done"), sem("wlat_done"), sem("A_lo_done")
        lat_ready, lat_hi_done, lat_lo_done = sem("lat_ready"), sem("lat_hi_done"), sem("lat_lo_done")
        q_ready, q_hi_done, q_copied, q_lo_done = sem("q_ready"), sem("q_hi_done"), sem("q_copied"), sem("q_lo_done")
        q_stacked = [[sem(f"q_stacked{i}_{t}") for t in range(NG)] for i in range(NBUF)]
        m_stacked = [sem(f"m_stacked{i}") for i in range(NBUF)]
        scores_ready, max_done = sem("scores_ready"), sem("max_done")
        mT_ready, mhi_done, m_done = sem("mT_ready"), sem("mhi_done"), sem("m_done")
        scoresT_ready, exp_done, masked, summed = sem("scoresT_ready"), sem("exp_done"), sem("masked"), sem("summed")
        o_ready, o_copied, d_ready, rden_done, rdb_done = sem("o_ready"), sem("o_copied"), sem("d_ready"), sem("rden_done"), sem("rdb_done")
        on_done, out_ready, x1_done = sem("on_done"), sem("out_ready"), sem("x1_done")

        def batches(eng, step):
            for u in range(NBUF):
                step(u, 0, u, 3)
            with eng.Fori(1, B // NBUF - 1) as r:
                for u in range(NBUF):
                    step(r * NBUF + u, r, u, 3)
            for i in range(B - 2 - NBUF, B):
                step(i, i // NBUF, i % NBUF, min(3, B - 1 - i))

        def query_banks(b, t):
            return SB_ if isinstance(b, int) and b == 0 and t % 2 else SA

        def score_banks(b, t):
            return SA if isinstance(b, int) and b == B - 1 and t % 2 else SB_

        def later(b, k):
            return not isinstance(b, int) or b >= k

        def turn(r, u, k):
            return r + (u + k) // NBUF, (u + k) % NBUF

        NH, RU, LAG = 4, 4, 2
        def columns(t, k):
            return t[:, 2 * k:2 * k + 2, :].rearrange("p a q -> p (a q)")

        assert (B - 3) % NBUF == 2 and CH == 2 * L and D * 2 == L and E * 2 == H
        w1_hi, w1_lo = [Qs[i][:, 0:E, :] for i in (2, 0)]
        w2_hi, w2_lo = [Qs[i][:, E:2 * E, :].rearrange("p a (b d) -> p (a b) d", b=2) for i in (2, 0)]
        x_hi = [columns(q_hi, u) for u in range(2)]
        x_lo = [columns(q_lo, u) for u in range(2)]
        h_hi = [columns(Qs[1], k) for k in range(NH)]
        h_lo = [columns(Qs[1], NH + k) for k in range(NH)]
        hid = [Pr[2][:, CH * k:CH * k + CH] for k in range(NH)]
        y = [Pr[3][:, CH * u:CH * u + CH].rearrange("p (j d) -> p j d", d=D) for u in range(2)]
        b1_rows = sb("b1_rows", [HC, P], F32)
        b1_col = sb("b1_col", [P, HC], F32)
        gw = sb("gw", [E, D], F32)
        gw_parts = sb("gw_parts", [P, 2, E], F32R)
        gate_rows = sb("gate_rows", [1, 2, E], F32)
        b2_rows = sb("b2_rows", [E, D], F32)
        ones = sb("ones", [E, P], F32)
        gate_bc = sb("gate_bc", [P, 2, E], F32)
        zero_col, gelu_of_zero = sb("zero_col", [P, 1]), sb("gelu_of_zero", [P, 1])
        b2_col = sb("b2_col", [D, 1], F32)
        mv2 = [sb(f"mv2_{u}", [P, CT, 2], F32) for u in range(2)]
        var_eps = sb("var_eps", [P, CT], F32)
        rstd2 = [sb(f"rstd2_{u}", [P, CT], F32) for u in range(2)]
        euler = sb("euler", [P, CT * E], F32)
        xn2 = sb("xn2", [P, CT, D], F32)
        yT = sb("yT", [P, CH], F32)
        lg = sb("lg", [P, CT, E], F32)
        lg2 = sb("lg2", [P, CT, E], F32)
        ms = sb("ms", [P, CT], F32)
        rms = sb("rms", [P, CT], F32)
        z = sb("z", [P, CT, E], F32)
        ez = sb("ez", [P, CT, E], F32)
        zmax = sb("zmax", [P, CT], F32)
        g = sb("g", [P, CT], F32)
        norm = [sb(f"norm{u}", [P, CT], F32) for u in range(2)]

        def bank_x(c):
            return SB_[:, 0, :] if after(c, 1) else banks[0][:, :]

        bank_y = SB_[:, 1, :]
        up_banks = [SB_[:, 2, :], SA[:, 0, :], SA[:, 1, :], SA[:, 2, :]]
        sum_banks = [banks[1], banks[0]]

        b1_in, gw_in, b2_in = sem("b1_in"), sem("gw_in"), sem("b2_in")
        small_ready, gwh_done, small_done, w_hi_done, w_lo_done = [sem(n_) for n_ in
            ("small_ready", "gwh_done", "small_done", "w_hi_done", "w_lo_done")]
        st2 = sb("st2", [P, CT, 6], F32)
        st2_done, aggrs_begun = sem("st2_done"), sem("aggrs_begun")
        fv = sem("fv")
        var_done, rstd2_done, xn2_done, xT2_ready, xhi_done, xlo_done = [sem(n_) for n_ in
            ("var_done", "rstd2_done", "xn2_done", "xT2_ready", "xhi_done", "xlo_done")]
        lg_ready, ms_done, rms_done, z_done, ez_done, norm_done = [sem(n_) for n_ in
            ("lg_ready", "ms_done", "rms_done", "z_done", "ez_done", "norm_done")]
        up_ready, hhi_done, hid_done, hlo_done, down_done = [sem(n_) for n_ in
            ("up_ready", "hhi_done", "hid_done", "hlo_done", "down_done")]
        gate_step, bias_added, yT_done, yT_turned, y_done = [sem(n_) for n_ in ("gate_step", "bias_added", "yT_done", "yT_turned", "y_done")]
        stored = [sem(f"stored{u}") for u in range(2)]

        def chunks(eng, step):
            for c in range(2):
                step(c, 0, c, True)
            with eng.Fori(1, NC // 2 - 1) as r:
                for u in range(2):
                    step(2 * r + u, r, u, True)
            for c in range(NC - 2, NC):
                step(c, c // 2, c % 2, c + 1 < NC)

        def after(c, k):
            return not isinstance(c, int) or c >= k

        with nc.Block() as block:
            @block.sync
            def _(sp):
                sp.dma_start(X[:, 0:FIRST, :], x_tiles[:, 0:FIRST, :]).then_inc(x_in[0], 16)
                sp.dma_start(wq_sb, Wq.rearrange("d h k -> d (h k)")).then_inc(wq_in, 16)
                sp.dma_start(wk_sb, Wk_up.rearrange("c h k -> c (h k)")).then_inc(wk_in, 16)
                sp.dma_start(wv_sb, Wv_up.rearrange("c h k -> c (h k)")).then_inc(wk_in, 16)
                sp.dma_start(X[:, FIRST:SQ, :], x_tiles[:, FIRST:SQ, :]).then_inc(x_in[1], 16)
                sp.dma_start(wo_sb, Wout.rearrange("(g a) k o -> (a k) g o", a=2)).then_inc(wo_in, 16)
                for n in range(1, 4):
                    sp.dma_start(X[:, SQ * n:SQ * n + SQ, :], x_tiles[:, SQ * n:SQ * n + SQ, :]).then_inc(x_in[n + 1], 16)
                sp.dma_start(w1_raw[:, :, :], w1.rearrange("e d f -> d e f")).then_inc(ffn_in, 16)
                sp.dma_start(w2_raw[:, :, :], w2.rearrange("e (a p) d -> p (e a) d", p=P)).then_inc(ffn_in, 16)
                sp.dma_start(gw[:, :], gate_w).then_inc(gw_in, 16)
                sp.dma_start(gate_rows[:, 0, :], gate_b.rearrange("(o e) -> o e", o=1)).then_inc(gw_in, 16)
                sp.dma_start(gate_rows[:, 1, :], rms_w.rearrange("(o e) -> o e", o=1)).then_inc(gw_in, 16)
                sp.dma_start(b2_rows[:, :], b2).then_inc(b2_in, 16)
                sp.dma_start(b1_rows[:, :], b1.rearrange("e (a p) -> (e a) p", p=P)).then_inc(b1_in, 16)

                def stack_q(b, r, u):
                    for k, src, done in ((0, q_hi, q_hi_done), (2, q_hi, q_hi_done), (1, q_lo, q_lo_done)):
                        sp.wait_ge(done, 2 * b + 2)
                        for t in range(NG):
                            sp.dma_start(Qs[u][k * C:(k + 1) * C, G * t:G * t + G, :].bitcast(F32),
                                         src[t * C:(t + 1) * C, :, :].bitcast(F32)).then_inc(q_stacked[u][t], 16)

                stack_q(0, 0, 0)
                stack_q(1, 0, 1)

                def step(i, r, u, ahead):
                    if ahead >= 2:
                        stack_q(i + 2, *turn(r, u, 2))
                batches(sp, step)

                def chunk_step(c, r, u, more):
                    sp.wait_ge(y_done, c + 1)
                    sp.dma_start(out_tiles[:, bass.ds(c * CT, CT), :], y[u][:, :, :]).then_inc(stored[u], 16)
                chunks(sp, chunk_step)
                for u in range(2):
                    sp.wait_ge(stored[u], 16 * (NC // 2))

            @block.gpsimd
            def _(pool):
                pool.memset(ident[:, :], 0.0).then_inc(zeroed, 1)
                pool.memset(mask[:, :], 0.0).then_inc(zeroed, 1)
                pool.memset(one_t[:, :, :], 1.0).then_inc(zeroed, 1)
                pool.memset(neg_half[:, :], -0.5).then_inc(zeroed, 1)
                pool.memset(zero_col[:, :], 0.0).then_inc(zeroed, 1)
                pool.memset(ones[:, :], 1.0).then_inc(zeroed, 1)
                pool.memset(euler[:, :], 2.718281828459045).then_inc(zeroed, 1)
                pool.wait_ge(zeroed, 7)
                pool.affine_select(out=ident[:, :], in_=ident[:, :], compare_op=ALU.not_equal, fill=1.0, base=0,
                                   pattern=[[-1, P]], channel_multiplier=1).then_inc(consts, 1)

                def root(first, n, ready):
                    pool.wait_ge(var_ready, ready)
                    pool.tensor_tensor(rstd[:, first:first + n], std[:, first:first + n], neg_half[:, 0:n],
                                       ALU.pow).then_inc(rstd_done, 1)

                root(0, FIRST, 1)
                pool.affine_select(out=mask[:, :], in_=mask[:, :], compare_op=ALU.is_ge, fill=MASKED, base=P,
                                   pattern=[[-1, L]], channel_multiplier=1).then_inc(consts, 1)
                W = C // NG
                pool.affine_select(out=one_t[:, :, :], in_=one_t[:, :, :], compare_op=ALU.is_ge, fill=0.0, base=0,
                                   pattern=[[-W, NG], [1, C]], channel_multiplier=0).then_inc(masks_set, 1)
                pool.wait_ge(masks_set, 1)
                pool.affine_select(out=one_t[:, :, :], in_=one_t[:, :, :], compare_op=ALU.is_ge, fill=0.0, base=W - 1,
                                   pattern=[[W, NG], [-1, C]], channel_multiplier=0).then_inc(consts, 1)
                def low_xT(b):
                    pool.wait_ge(xT_copied, b + 1)
                    pool.tensor_tensor(xT_lo[:, :], xnT[:, :], xT_hi[:, :].bitcast(F32), ALU.subtract).then_inc(xT_lo_done, 1)

                low_xT(0)
                root(FIRST, SQ - FIRST, 2)
                low_xT(1)
                root(SQ, SQ, 4)

                def mask_probs(b, t, u):
                    pool.wait_ge(exp_done, NG * b + t + 1)
                    pool.sem_inc(selects_begun, 1)
                    blocks = Pr[(NG * u + t) % PR][:, :].rearrange("p (n q) -> p n q", q=P)
                    for part in (blocks[:, 0:2 * G:2, :], blocks[:, 2 * G:3 * G, :]):
                        ins = pool.affine_select(out=part, in_=part, compare_op=ALU.is_ge, fill=0.0, base=0,
                                                 pattern=[[0, G], [1, P]], channel_multiplier=-1)
                    ins.then_inc(masked, 1)

                def sum_probs(b, t, u):
                    blocks = Pr[(NG * u + t) % PR][:, :].rearrange("p (n q) -> p n q", q=P)
                    pool.wait_ge(masked, NG * b + t + 1)
                    pool.tensor_tensor(blocks[:, 3 * G:4 * G, :], blocks[:, 1:2 * G:2, :], blocks[:, 2 * G:3 * G, :],
                                       ALU.add).then_inc(summed, 1)

                def divide(b):
                    pool.wait_ge(o_copied, NG * b + NG)
                    pool.wait_ge(rdb_done, b + 1)
                    if later(b, 1):
                        pool.wait_ge(out_ready, b)
                    pool.tensor_tensor(On[:, :, :], O[:, :, :], rdb[:, :, :], ALU.mult).then_inc(on_done, 1)

                def rsqrt_var(c, u):
                    pool.wait_ge(var_done, c + 1)
                    pool.tensor_tensor(rstd2[u][:, :], var_eps[:, :], neg_half[:, 0:CT], ALU.pow).then_inc(rstd2_done, 1)

                def gates(c):
                    pool.wait_ge(ms_done, c + 1)
                    pool.tensor_tensor(rms[:, :], ms[:, :], neg_half[:, 0:CT], ALU.pow).then_inc(rms_done, 1)
                    pool.wait_ge(z_done, c + 1)
                    pool.tensor_tensor(ez[:, :, :].rearrange("p j e -> p (j e)"), euler[:, :],
                                       z[:, :, :].rearrange("p j e -> p (j e)"), ALU.pow).then_inc(ez_done, 1)

                def step(i, r, u, ahead):
                    if ahead == 1:
                        rsqrt_var(0, 0)
                    if ahead >= 2:
                        low_xT(i + 2)
                    mask_probs(i, 0, u)
                    sum_probs(i, 0, u)
                    mask_probs(i, 1, u)
                    if later(i, 1):
                        divide(i - 1)
                    mask_probs(i, 2, u)
                    sum_probs(i, 1, u)
                    sum_probs(i, 2, u)
                    mask_probs(i, 3, u)
                    if isinstance(i, int) and i in (1, 2):
                        root(SQ * (i + 1), SQ, 4 * i + 3)
                batches(pool, step)
                divide(B - 1)

                gates(0)

                def chunk_step(c, r, u, more):
                    if more:
                        rsqrt_var(c + 1, 1 - u)
                        gates(c + 1)
                chunks(pool, chunk_step)

            @block.scalar
            def _(act):
                act.dma_start(wlat[:, :], Wkv).then_inc(lat_in, 16)
                act.wait_ge(wT_ready, 1)
                act.wait_ge(k_zeroed, 1)
                act.wait_ge(zeroed, 7)
                act.activation(wqT, SB_[:, 0:2, :].rearrange("p a (g d) -> p (a g) d", d=D), ACT.Copy).then_inc(wT_copied, 1)
                for s in range(2):
                    half = slice(HD * s, HD * s + HD)
                    act.activation(wkT[half, :, s, :], SB_[half, 2, 0:H // 2 * C].rearrange("p (g c) -> p g c", c=C),
                                   ACT.Copy).then_inc(wT_copied, 1)
                act.activation(wvT, SB_[:, 2, H // 2 * C:H * C].rearrange("p (g c) -> p g c", c=C), ACT.Copy).then_inc(v_copied, 1)

                def copy_A():
                    act.wait_ge(A_ready, 1)
                    act.activation(A_hi[:, :, :].rearrange("p h c -> p (h c)"), SA[:, 0, :], ACT.Copy, scale=float(HD) ** -0.5)
                    act.activation(A_full, SA[:, 0, :], ACT.Copy, scale=float(HD) ** -0.5).then_inc(A_copied, 1)

                def copy_vo():
                    act.wait_ge(vo_ready, 1)
                    for s in range(2):
                        ins = act.activation(Wvo[:, s::2, :], SB_[:, s, 0:NG // 2 * D].rearrange("p (t o) -> p t o", o=D), ACT.Copy)
                    ins.then_inc(vo_copied, 1)

                def copy_xT(b):
                    act.wait_ge(xT_ready, b + 1)
                    act.activation(xT_hi[:, :], banks[0][:, 0:L], ACT.Copy)
                    act.activation(xnT[:, :], banks[0][:, 0:L], ACT.Copy).then_inc(xT_copied, 1)

                def high_latents(b, u):
                    act.wait_ge(lat_ready, b + 1)
                    act.activation(Ls[u][0:KS, :], banks[0][0:KS, 0:L], ACT.Copy)
                    act.activation(Ln[u][:, :, :].rearrange("p s c -> p (s c)"), banks[0][:, L:L + QT * C],
                                   ACT.Copy).then_inc(lat_hi_done, 1)

                def high_queries(b, before):
                    if before is not None:
                        for t in range(NG):
                            act.wait_ge(q_stacked[before[1]][t], 16 * 3 * (before[0] + 1))
                    for dst, done in ((q_hi, q_hi_done), (q, q_copied)):
                        for k in range(2):
                            act.wait_ge(q_ready, 2 * b + k + 1)
                            act.activation(dst[:, 2 * k:2 * k + 2, :].rearrange("p t q -> p (t q)"), banks[1 - k][:, :],
                                           ACT.Copy).then_inc(done, 1)

                def stack_m(b, r, u):
                    act.wait_ge(m_done, b + 1)
                    for k, src in enumerate((m_hi, m_lo)):
                        act.dma_start(Qs[u][KS + k:KS + k + 1, :, :].rearrange("o h (s q) -> o (h s) q", q=P).bitcast(F32),
                                     src[:, :].bitcast(F32)).then_inc(m_stacked[u], 16)

                def copy_o(b, t):
                    act.wait_ge(o_ready, NG * b + t + 1)
                    if later(b, 1):
                        act.wait_ge(on_done, b)
                    act.activation(O[:, t, :], banks[int(t != 1)][:, 0:L], ACT.Copy).then_inc(o_copied, 1)

                def exps(b, t, u):
                    act.wait_ge(scoresT_ready, NG * b + t + 1)
                    if t >= 2 and later(b, 1):
                        act.wait_ge(d_ready, b)
                    if t < 2 and later(b, 2):
                        act.wait_ge(d_ready, b - 1)
                    bank = score_banks(b, t)
                    act.activation(Pr[(NG * u + t) % PR][:, 0:PG], bank[:, :, :].rearrange("p a q -> p (a q)"), ACT.Exp).then_inc(exp_done, 1)

                copy_xT(0)
                high_latents(0, 0)
                copy_A()
                high_queries(0, None)
                copy_vo()
                copy_xT(1)
                high_latents(1, 1)
                high_queries(1, (0, 0))

                def high_x(c, u):
                    act.wait_ge(xT2_ready, c + 1)
                    act.activation(x_hi[u], bank_x(c), ACT.Copy).then_inc(xhi_done, 1)

                stack_m(0, 0, 0)

                def step(i, r, u, ahead):
                    if ahead >= 2:
                        copy_xT(i + 2)
                    exps(i, 0, u)
                    if ahead == 1:
                        act.wait_ge(ffn_in, 32)
                        act.activation(w1_hi, w1_raw[:, :, :], ACT.Copy).then_inc(w_hi_done, 1)
                    if not ahead:
                        high_x(0, 0)
                    if ahead >= 2:
                        high_latents(i + 2, (u + 2) % NBUF)
                    exps(i, 1, u)
                    if ahead == 1:
                        act.activation(w2_hi, w2_raw[:, :, :], ACT.Copy).then_inc(w_hi_done, 1)
                        act.wait_ge(small_done, 1)
                    if ahead >= 2:
                        high_queries(i + 2, turn(r, u, 1))
                    exps(i, 2, u)
                    copy_o(i, 0)
                    copy_o(i, 1)
                    exps(i, 3, u)
                    if not ahead:
                        act.activation(gelu_of_zero[:, :], zero_col[:, :], ACT.Gelu)
                    copy_o(i, 2)
                    if ahead:
                        stack_m(i + 1, *turn(r, u, 1))
                    copy_o(i, 3)
                batches(act, step)

                def chunk_step(c, r, u, more):
                    for k in range(HC):
                        if more and k == 10:
                            high_x(c + 1, 1 - u)
                        act.wait_ge(up_ready, HC * c + k + 1)
                        if k >= NH or after(c, 1):
                            act.wait_ge(down_done, HC * c + k + 1 - NH)
                        act.activation(h_hi[k % NH][:, :], up_banks[k % RU], ACT.Gelu,
                                       bias=b1_col[:, k:k + 1]).then_inc(hhi_done, 1)
                        act.activation(hid[k % NH][:, :], up_banks[k % RU], ACT.Gelu,
                                       bias=b1_col[:, k:k + 1]).then_inc(hid_done, 1)
                chunks(act, chunk_step)

            @block.vector
            def _(dve):
                dve.memset(wkT, 0.0).then_inc(k_zeroed, 1)
                for u in range(NBUF):
                    ins = dve.memset(Ls[u][KS:P, :].bitcast(F32), -1.0)
                ins.then_inc(ones_set, 1)
                def token_stats(piece, load, first, n):
                    dve.wait_ge(x_in[load], 16)
                    for k in range(first, first + n):
                        ins = dve.bn_stats(stats[:, k, :], X[:, k, :])
                    ins.then_inc(stats_done, 1)
                    dve.wait_ge(stats_done, piece + 1)
                    for k in range(first, first + n):
                        ins = dve.bn_aggr(mv[:, k, :], stats[:, k, :])
                    ins.then_inc(aggr_done, 1)
                    dve.wait_ge(aggr_done, piece + 1)
                    dve.tensor_scalar(std[:, first:first + n], mv[:, first:first + n, 1], EPS, None,
                                      ALU.add).then_inc(var_ready, 1)

                def normalize(b):
                    if later(b, 1):
                        dve.wait_ge(xT_ready, b)
                    for s in range(QT):
                        n = bass.ds(b * QT + s, 1)
                        ins = dve.tensor_scalar(xn[:, s, :], X[:, n, :].rearrange("p o d -> p (o d)"),
                                                mv[:, n, 0:1].rearrange("p o d -> p (o d)"), rstd[:, n],
                                                ALU.subtract, ALU.mult)
                    ins.then_inc(xn_ready, 1)

                def low_latents(b, u):
                    dve.wait_ge(lat_hi_done, b + 1)
                    dve.tensor_tensor(Ls[u][2 * C:KS, :], banks[0][2 * C:KS, 0:L], Ls[u][2 * C:KS, :].bitcast(F32),
                                      ALU.subtract).then_inc(lat_lo_done, 1)

                def low_queries(b):
                    for k in range(2):
                        dve.wait_ge(q_copied, 2 * b + k + 1)
                        dve.tensor_tensor(q_lo[:, 2 * k:2 * k + 2, :].rearrange("p t q -> p (t q)"),
                                          q[:, 2 * k:2 * k + 2, :].rearrange("p t q -> p (t q)"),
                                          q_hi[:, 2 * k:2 * k + 2, :].rearrange("p t q -> p (t q)").bitcast(F32),
                                          ALU.subtract).then_inc(q_lo_done, 1)

                def maxima(b, t):
                    bank = query_banks(b, t)
                    if t == 0 and later(b, 1):
                        dve.wait_ge(mT_ready, b)
                    for a_ in range(3):
                        dve.wait_ge(scores_ready, 3 * (NG * b + t) + a_ + 1)
                        dve.sem_inc(maxima_begun, 1)
                        for j in range(G) if a_ == 0 else range(2 * a_ - 2, 2 * a_):
                            if a_ == 0:
                                part, late = bank[:, 0, j * P:j * P + P], mask[:, P:L]
                            else:
                                part, late = bank[:, a_, j % 2 * L:j % 2 * L + L], mask[:, :]
                            ins = dve.tensor_tensor_reduce(part, part, late, 1.0, MASKED, ALU.add, ALU.max,
                                                           qmax[:, G * t + j, min(a_, 1):min(a_, 1) + 1])
                        ins.then_inc(max_done, 1)

                def split_max(b, r, u):
                    dve.wait_ge(mT_ready, b + 1)
                    if later(b, 1):
                        rr, uu = turn(r, u, -1)
                        dve.wait_ge(m_stacked[uu], 32 * (rr + 1))
                    dve.tensor_copy(m_hi[:, :], SA[0:H * QT, 0, 0:P]).then_inc(mhi_done, 1)
                    dve.wait_ge(mhi_done, b + 1)
                    dve.tensor_tensor(m_lo[:, :], SA[0:H * QT, 0, 0:P], m_hi[:, :].bitcast(F32), ALU.subtract).then_inc(m_done, 1)

                def invert_sums(b):
                    dve.wait_ge(d_ready, b + 1)
                    if later(b, 1):
                        dve.wait_ge(rdb_done, b)
                    dve.reciprocal(rden[:, :], banks[0][:, 0:L]).then_inc(rden_done, 1)

                def spread_sums(b):
                    dve.wait_ge(rden_done, b + 1)
                    if later(b, 1):
                        dve.wait_ge(on_done, b)
                    dve.sem_inc(shuffles_begun, 1)
                    for t in range(NG):
                        ins = dve.stream_shuffle(rdb[:, t, :], rden[:, :], [C // NG * t] * 32)
                    ins.then_inc(rdb_done, 1)

                def residual(b):
                    dve.wait_ge(out_ready, b + 1)
                    xb = X[:, bass.ds(b * QT, QT), :]
                    dve.tensor_tensor(xb, banks[0][:, 0:L].rearrange("p (s d) -> p s d", d=D), xb, ALU.add).then_inc(x1_done, 1)

                def chunk_stats(c, u):
                    for k in range(CT):
                        n = bass.ds(c * CT + k, 1)
                        ins = dve.bn_stats(st2[:, k, :], X[:, n, :].rearrange("p o d -> p (o d)"))
                    ins.then_inc(st2_done, 1)
                    dve.wait_ge(st2_done, c + 1)
                    dve.sem_inc(aggrs_begun, 1)
                    for k in range(CT):
                        ins = dve.bn_aggr(mv2[u][:, k, :], st2[:, k, :])
                    ins.then_inc(fv, 1)
                    dve.wait_ge(fv, 6 * c + 1)
                    dve.tensor_scalar(var_eps[:, :], mv2[u][:, :, 1], EPS, None, ALU.add).then_inc(var_done, 1)

                def normalize_chunk(c, u):
                    dve.wait_ge(rstd2_done, c + 1)
                    if after(c, 1):
                        dve.wait_ge(xT2_ready, c)
                    for k in range(CT):
                        n = bass.ds(c * CT + k, 1)
                        ins = dve.tensor_scalar(xn2[:, k, :], X[:, n, :].rearrange("p o d -> p (o d)"), mv2[u][:, k, 0:1],
                                                rstd2[u][:, k:k + 1], ALU.subtract, ALU.mult)
                    ins.then_inc(xn2_done, 1)

                def low_x(c, u):
                    dve.wait_ge(xhi_done, c + 1)
                    dve.tensor_tensor(x_lo[u], bank_x(c), x_hi[u].bitcast(F32), ALU.subtract).then_inc(xlo_done, 1)

                def gate_in(c):
                    dve.wait_ge(lg_ready, c + 1)
                    parts = bank_x(c)[:, 0:CT * 2 * E].rearrange("p (j a e) -> p j a e", a=2, e=E)
                    dve.tensor_tensor(lg2[:, :, :], parts[:, :, 0, :], gate_bc[:, 0:1, :].to_broadcast([P, CT, E]),
                                      ALU.add).then_inc(bias_added, 1)
                    dve.wait_ge(bias_added, c + 1)
                    dve.tensor_tensor(lg[:, :, :], lg2[:, :, :], parts[:, :, 1, :], ALU.add).then_inc(fv, 1)
                    dve.wait_ge(fv, 6 * c + 2)
                    dve.tensor_tensor(lg2[:, :, :], lg[:, :, :], lg[:, :, :], ALU.mult).then_inc(fv, 1)
                    dve.wait_ge(fv, 6 * c + 3)
                    dve.tensor_reduce(g[:, :], lg2[:, :, :], axis=AX.X, op=ALU.add).then_inc(fv, 1)
                    dve.wait_ge(fv, 6 * c + 4)
                    dve.tensor_scalar(ms[:, :], g[:, :], 1.0 / E, 1.1920928955078125e-07, ALU.mult, ALU.add).then_inc(ms_done, 1)

                def gate_max(c):
                    dve.wait_ge(rms_done, c + 1)
                    dve.tensor_tensor(lg2[:, :, :], lg[:, :, :], rms[:, :].unsqueeze(2).to_broadcast([P, CT, E]), ALU.mult).then_inc(fv, 1)
                    dve.wait_ge(fv, 6 * c + 5)
                    dve.tensor_tensor(lg[:, :, :], lg2[:, :, :], gate_bc[:, 1:2, :].to_broadcast([P, CT, E]), ALU.mult).then_inc(fv, 1)
                    dve.wait_ge(fv, 6 * c + 6)
                    dve.tensor_reduce(zmax[:, :], lg[:, :, :], axis=AX.X, op=ALU.max).then_inc(gate_step, 1)
                    dve.wait_ge(gate_step, 5 * c + 1)
                    dve.tensor_tensor(z[:, :, :], lg[:, :, :], zmax[:, :].unsqueeze(2).to_broadcast([P, CT, E]), ALU.subtract).then_inc(z_done, 1)

                def gate_out(c, u):
                    dve.wait_ge(ez_done, c + 1)
                    dve.tensor_reduce(ms[:, :], ez[:, :, :], axis=AX.X, op=ALU.add).then_inc(gate_step, 1)
                    dve.wait_ge(gate_step, 5 * c + 2)
                    dve.reciprocal(g[:, :], ms[:, :]).then_inc(gate_step, 1)
                    dve.wait_ge(gate_step, 5 * c + 3)
                    dve.tensor_scalar(zmax[:, :], g[:, :], 1e-06, None, ALU.add).then_inc(gate_step, 1)
                    dve.wait_ge(gate_step, 5 * c + 4)
                    dve.reciprocal(ms[:, :], zmax[:, :]).then_inc(gate_step, 1)
                    dve.wait_ge(gate_step, 5 * c + 5)
                    dve.tensor_tensor(norm[u][:, :], g[:, :], ms[:, :], ALU.mult).then_inc(norm_done, 1)

                def low_hidden(c, k):
                    dve.wait_ge(hid_done, HC * c + k + 1)
                    dve.tensor_tensor(h_lo[k % NH], hid[k % NH], h_hi[k % NH].bitcast(F32),
                                      ALU.subtract).then_inc(hlo_done, 1)

                def add_bias(c, u):
                    dve.wait_ge(down_done, HC * c + HC)
                    if after(c, 1):
                        dve.wait_ge(yT_turned, c)
                    dve.tensor_scalar(yT[:, :], sum_banks[u][:, :], b2_col[:, :], None, ALU.add).then_inc(yT_done, 1)

                def finish(c, r, u):
                    dve.wait_ge(yT_turned, c + 1)
                    if after(c, 2):
                        dve.wait_ge(stored[u], 16 * r)
                    dve.wait_ge(norm_done, c + 1)
                    for k in range(CT):
                        n = bass.ds(c * CT + k, 1)
                        ins = dve.scalar_tensor_tensor(y[u][:, k, :], bank_y[:, k * D:k * D + D], norm[u][:, k:k + 1],
                                                       X[:, n, :].rearrange("p o d -> p (o d)"), ALU.mult, ALU.add)
                    ins.then_inc(y_done, 1)

                def low_weights(k):
                    dve.wait_ge(w_hi_done, k + 1)
                    raw, high, low = ((w1_raw, w1_hi, w1_lo), (w2_raw, w2_hi, w2_lo))[k]
                    dve.tensor_tensor(low, raw[:, :, :], high.bitcast(F32), ALU.subtract).then_inc(w_lo_done, 1)

                def small_weights():
                    dve.wait_ge(small_ready, 1)
                    dve.tensor_copy(gw_parts[:, 0, :], banks[0][:, HC:HC + E]).then_inc(gwh_done, 1)
                    dve.wait_ge(gwh_done, 1)
                    dve.tensor_tensor(gw_parts[:, 1, :], banks[0][:, HC:HC + E], gw_parts[:, 0, :].bitcast(F32), ALU.subtract)
                    dve.tensor_copy(gate_bc[:, 0, :], banks[0][:, HC + E:HC + 2 * E])
                    dve.tensor_scalar(gate_bc[:, 1, :], banks[0][:, HC + 2 * E:HC + 3 * E], 2.0, None, ALU.mult)
                    dve.tensor_copy(b1_col[:, :], banks[0][:, 0:HC])
                    dve.tensor_copy(b2_col[:, :], banks[0][:, D:D + 1]).then_inc(small_done, 1)

                dve.wait_ge(lat_in, 16)
                thrice = wlat[:, :].unsqueeze(1).to_broadcast([P, 3, C])
                dve.tensor_copy(wlat_hi[:, :, :], thrice).then_inc(wlat_hi_done, 1)
                dve.wait_ge(wlat_hi_done, 1)
                dve.tensor_tensor(wlat_lo[:, :, :], thrice, wlat_hi[:, :, :].bitcast(F32), ALU.subtract).then_inc(wlat_done, 1)
                token_stats(0, 0, 0, FIRST)
                dve.wait_ge(rstd_done, 1)
                normalize(0)
                normalize(1)
                low_latents(0, 0)
                token_stats(1, 1, FIRST, SQ - FIRST)
                dve.wait_ge(A_copied, 1)
                dve.tensor_tensor(A_lo[:, :, :].rearrange("p h c -> p (h c)"), A_full,
                                  A_hi[:, :, :].rearrange("p h c -> p (h c)").bitcast(F32), ALU.subtract).then_inc(A_lo_done, 1)
                low_queries(0)
                token_stats(2, 2, SQ, SQ // 2)
                low_latents(1, 1)
                token_stats(3, 2, SQ + SQ // 2, SQ // 2)
                token_stats(4, 3, 2 * SQ, SQ // 2)
                low_queries(1)
                dve.wait_ge(rstd_done, 2)
                normalize(2)
                dve.wait_ge(consts, 3)
                for t in range(NG):
                    maxima(0, t)
                split_max(0, 0, 0)

                def late_stats(p):
                    first = 2 * SQ + SQ // 2 + SQ // 4 * p
                    token_stats(5 + p, 1 + first // SQ, first, SQ // 4)

                def step(i, r, u, ahead):
                    if later(i, 1):
                        invert_sums(i - 1)
                    for t in range(NG):
                        if ahead:
                            maxima(i + 1, t)
                        if t == 0 and later(i, 1):
                            spread_sums(i - 1)
                        if t == 0 and not later(i, 1):
                            for p in range(3):
                                late_stats(p)
                        if t == 0 and ahead >= 2:
                            low_latents(i + 2, (u + 2) % NBUF)
                        if t == 2 and ahead >= 2:
                            low_queries(i + 2)
                        if t == 1 and ahead == 1:
                            small_weights()
                        if t == 2 and ahead == 2:
                            chunk_stats(0, 0)
                        if t == 2 and ahead == 1:
                            normalize_chunk(0, 0)
                        if t == 1 and not ahead:
                            low_x(0, 0)
                            dve.wait_ge(small_done, 1)
                            gate_in(0)
                            low_weights(0)
                        if t == 3 and not ahead:
                            low_weights(1)
                    if later(i, 1):
                        residual(i - 1)
                    if ahead:
                        split_max(i + 1, *turn(r, u, 1))
                    if ahead >= 3:
                        if later(i, NBUF):
                            dve.wait_ge(rstd_done, 5)
                        normalize(i + 3)
                    if not later(i, 3):
                        late_stats(3 + i)
                batches(dve, step)
                invert_sums(B - 1)
                spread_sums(B - 1)

                def chunk_step(c, r, u, more):
                    for k in range(HC):
                        if k == 2 and after(c, 1):
                            add_bias(c - 1, 1 - u)
                        if more and k == 4:
                            chunk_stats(c + 1, 1 - u)
                        if k == 6 and after(c, 1):
                            finish(c - 1, r - (1 - u), 1 - u)
                        if more and k == 8:
                            normalize_chunk(c + 1, 1 - u)
                        if k == 3 and not after(c, 1):
                            gate_max(0)
                        if k == 7 and not after(c, 1):
                            residual(B - 1)
                        if k == 10:
                            gate_out(c, u)
                        if more and k == 11:
                            low_x(c + 1, 1 - u)
                        if more and k == 13:
                            gate_in(c + 1)
                        if more and k == 14:
                            gate_max(c + 1)
                        low_hidden(c, k)
                chunks(dve, chunk_step)
                add_bias(NC - 1, 1)
                finish(NC - 1, NC // 2 - 1, 1)

            @block.tensor
            def _(pe):
                pe.wait_ge(consts, 1)
                pe.wait_ge(wq_in, 16)
                for g in range(H // 2):
                    pe.transpose(SB_[:, g // 4, g % 4 * D:g % 4 * D + D], wq_sb[:, g * P:g * P + P], ident[:, :])
                pe.wait_ge(wk_in, 32)
                for v, w in enumerate((wk_sb, wv_sb)):
                    for g in range(H // 2):
                        at = (v * H // 2 + g) * C
                        ins = pe.transpose(SB_[:, 2, at:at + C], w[:, g * P:g * P + P], ident[0:C, 0:C])
                ins.then_inc(wT_ready, 1)

                def weights_A():
                    pe.wait_ge(wT_copied, 3)
                    for g in range(H // 2):
                        ins = pe.matmul(SA[:, 0, g * 2 * C:g * 2 * C + 2 * C], wqT[:, g, :],
                                        wkT[:, g, :, :].rearrange("p s c -> p (s c)"), start=True, stop=True)
                    ins.then_inc(A_ready, 1)

                def weights_vo():
                    pe.wait_ge(wo_in, 16)
                    pe.wait_ge(v_copied, 1)
                    for h in range(H):
                        g, s, t, j = h // 2, h % 2, h % G, h // G
                        rows = slice(HD * s, HD * s + HD)
                        ins = pe.matmul(SB_[C * j:C * j + C, s, t // 2 * D:t // 2 * D + D], wvT[rows, g, :], wo_sb[rows, g, :],
                                        start=True, stop=True)
                    ins.then_inc(vo_ready, 1)

                def transpose_x(b):
                    pe.wait_ge(xn_ready, b + 1)
                    for s in range(QT):
                        ins = pe.transpose(banks[0][:, s * P:s * P + P], xn[:, s, :], ident[:, :])
                    ins.then_inc(xT_ready, 1)

                def latents_by_token(b):
                    pe.wait_ge(xT_copied, b + 1)
                    for s in range(QT):
                        pe.matmul(banks[0][:, L + s * C:L + s * C + C], xnT[:, s * P:s * P + P], wlat[:, :],
                                  start=True, stop=True)

                def latents(b):
                    pe.wait_ge(xT_lo_done, b + 1)
                    for m, (w, xs) in enumerate(((wlat_hi, xT_hi), (wlat_lo, xT_hi), (wlat_hi, xT_lo))):
                        ins = pe.matmul(banks[0][0:KS, 0:L], w[:, :, :].rearrange("p k c -> p (k c)"), xs[:, :],
                                        start=(m == 0), stop=(m == 2))
                    ins.then_inc(lat_ready, 1)

                def queries(b, k):
                    for t in range(2 * k, 2 * k + 2):
                        for m, (w, xs) in enumerate(((A_hi, xT_hi), (A_lo, xT_hi), (A_hi, xT_lo))):
                            ins = pe.matmul(banks[1 - k][:, t % 2 * L:t % 2 * L + L],
                                            w[:, G * t:G * t + G, :].rearrange("p h c -> p (h c)"), xs[:, :],
                                            start=(m == 0), stop=(m == 2))
                    ins.then_inc(q_ready, 1)

                def scores(b, t, u, some=(0, 1, 2)):
                    bank = query_banks(b, t)
                    before = 2 if isinstance(b, int) and b == 0 else 1
                    for a_ in some:
                        if t >= before or later(b, 1):
                            pe.wait_ge(max_done, 3 * (NG * b + t - before) + a_ + 1)
                        if t == 0 and a_ == 0 and later(b, 1):
                            pe.wait_ge(m_done, b)
                        for j in range(G) if a_ == 0 else range(2 * a_ - 2, 2 * a_):
                            h = G * t + j
                            if a_ == 0:
                                ins = pe.matmul(bank[:, 0, j * P:j * P + P], Qs[u][0:KS, h, 0:P], Ls[u][0:KS, 0:P],
                                                start=True, stop=True)
                            else:
                                ins = pe.matmul(bank[:, a_, j % 2 * L:j % 2 * L + L], Qs[u][0:KS, h, P:L], Ls[u][0:KS, :],
                                                start=True, stop=True)
                        ins.then_inc(scores_ready, 1)

                def scores_T(b, t, u):
                    K = KS + 2
                    bank = score_banks(b, t)
                    for a_ in range(2):
                        h = G * t + 2 * a_
                        pe.matmul(bank[:, a_, :], Ls[u][0:K, 0:P], Qs[u][0:K, h:h + 2, :].rearrange("p h q -> p (h q)"),
                                  start=True, stop=True)
                    pe.matmul(bank[:, 2, :], Ls[u][0:K, P:L], Qs[u][0:K, G * t:G * t + G, P:L],
                              start=True, stop=True).then_inc(scoresT_ready, 1)

                def parts(u, t):
                    p = Pr[(4 * u + t) % PR]
                    for j in range(G):
                        yield 0, j, p[:, j * L:j * L + L], slice(0, L)
                    for j in range(G):
                        yield 1, j, p[:, G * L + j * P:G * L + j * P + P], slice(P, L)

                def weigh(b, t, u, bank):
                    pe.wait_ge(masked, NG * b + t + 1)
                    for s, j, p, q in parts(u, t):
                        ins = pe.matmul(bank[C * j:C * j + C, q], Ln[u][:, s, :], p, start=(s == 0), stop=(s == 1),
                                        skip_group_check=True)
                    ins.then_inc(o_ready, 1)

                def sums(b, u, bank):
                    for t in range(NG):
                        if t < NG - 1:
                            pe.wait_ge(summed, (NG - 1) * b + t + 1)
                            blocks = Pr[(NG * u + t) % PR][:, :].rearrange("p (n q) -> p n q", q=P)
                            for j in range(G):
                                last = 3 * G + j
                                pe.matmul(bank[C * j:C * j + C, 0:L], one_t[:, t, :], blocks[:, 2 * j:last + 1:last - 2 * j, :],
                                          start=(t == 0), stop=False, skip_group_check=True)
                        else:
                            pe.wait_ge(masked, NG * b + t + 1)
                            for s, j, p, q in parts(u, t):
                                ins = pe.matmul(bank[C * j:C * j + C, q], one_t[:, t, :], p, start=False, stop=(s == 1),
                                                skip_group_check=True)
                            ins.then_inc(d_ready, 1)

                def project(b, bank):
                    pe.wait_ge(on_done, b + 1)
                    for s in range(QT):
                        for t in range(NG):
                            ins = pe.matmul(bank[:, s * D:s * D + D], On[:, t, s * P:s * P + P], Wvo[:, t, :],
                                            start=(t == 0), stop=(t == NG - 1))
                    ins.then_inc(out_ready, 1)

                def transpose_max(b):
                    pe.wait_ge(max_done, 3 * NG * (b + 1))
                    pe.transpose(SA[0:H * QT, 0, 0:P], qmax[:, :, :].rearrange("p h s -> p (h s)"),
                                 ident[:, :]).then_inc(mT_ready, 1)

                def transpose_chunk(c):
                    pe.wait_ge(xn2_done, c + 1)
                    if after(c, 1):
                        pe.wait_ge(ms_done, c)
                    for k in range(CT):
                        ins = pe.transpose(bank_x(c)[:, k * P:k * P + P], xn2[:, k, :], ident[:, :])
                    ins.then_inc(xT2_ready, 1)

                def logits(c, u):
                    pe.wait_ge(xlo_done, c + 1)
                    for k in range(CT):
                        tok = slice(k * P, k * P + P)
                        at = k * 2 * E
                        pe.matmul(bank_x(c)[:, at:at + 2 * E], x_hi[u][:, tok], gw_parts[:, :, :].rearrange("p a e -> p (a e)"),
                                  start=True, stop=False, skip_group_check=True)
                        ins = pe.matmul(bank_x(c)[:, at:at + E], x_lo[u][:, tok], gw_parts[:, 0, :], start=False, stop=True,
                                        skip_group_check=True)
                    ins.then_inc(lg_ready, 1)

                def up(c, k, u):
                    if k >= RU or after(c, 1):
                        pe.wait_ge(hid_done, HC * c + k + 1 - RU)
                    unit = slice(k % 2 * P, k % 2 * P + P)
                    for m, (ws, xs) in enumerate(((w1_hi, x_hi), (w1_lo, x_hi), (w1_hi, x_lo))):
                        ins = pe.matmul(up_banks[k % RU], ws[:, k // 2, unit], xs[u], start=(m == 0), stop=(m == 2))
                    ins.then_inc(up_ready, 1)

                def down(c, k, u):
                    pe.wait_ge(hid_done, HC * c + k + 1)
                    pe.wait_ge(hlo_done, HC * c + k + 1)
                    for m, (ws, hs) in enumerate(((w2_hi, h_hi), (w2_lo, h_hi), (w2_hi, h_lo))):
                        ins = pe.matmul(sum_banks[u][:, :], ws[:, k, :], hs[k % NH], start=(k == 0 and m == 0),
                                        stop=(k == HC - 1 and m == 2))
                    ins.then_inc(down_done, 1)

                def turn_y(c):
                    pe.wait_ge(yT_done, c + 1)
                    if after(c, 1):
                        pe.wait_ge(y_done, c)
                    for j in range(CT):
                        ins = pe.transpose(bank_y[:, j * D:j * D + D], yT[:, j * P:j * P + P], ident[:, :])
                    ins.then_inc(yT_turned, 1)

                def turn_small():
                    pe.wait_ge(gw_in, 48)
                    pe.wait_ge(b2_in, 16)
                    pe.wait_ge(b1_in, 16)
                    pe.transpose(banks[0][:, 0:HC], b1_rows[:, :], ident[0:HC, 0:HC])
                    pe.transpose(banks[0][:, HC:HC + E], gw[:, :], ident[0:E, 0:E])
                    pe.matmul(banks[0][:, HC + E:HC + 3 * E], ones[0:1, :], gate_rows[:, :, :].rearrange("o a e -> o (a e)"), start=True, stop=True)
                    pe.matmul(banks[0][:, D:D + 1], b2_rows[:, :], ones[:, 0:1], start=True, stop=True).then_inc(small_ready, 1)

                transpose_x(0)
                pe.wait_ge(wlat_done, 1)
                latents_by_token(0)
                latents(0)
                weights_A()
                pe.wait_ge(A_lo_done, 1)
                queries(0, 0)
                pe.wait_ge(lat_lo_done, 1)
                queries(0, 1)
                weights_vo()
                pe.wait_ge(q_copied, 2)
                transpose_x(1)
                latents_by_token(1)
                latents(1)
                queries(1, 0)
                pe.wait_ge(lat_lo_done, 2)
                queries(1, 1)
                pe.wait_ge(ones_set, 1)
                pe.wait_ge(vo_copied, 1)
                for t in range(NG):
                    pe.wait_ge(q_stacked[0][t], 16 * 3)
                    scores(0, t, 0)
                transpose_max(0)
                pe.wait_ge(q_copied, 4)

                def step(i, r, u, ahead):
                    r1, u1 = turn(r, u, 1)
                    for t in range(NG):
                        if ahead:
                            if not (t == 1 and ahead >= 2):
                                pe.wait_ge(q_stacked[u1][t], 16 * 3 * (r1 + 1))
                            if t == 0:
                                scores(i + 1, t, u1)
                            elif t == 1:
                                scores(i + 1, t, u1, (2,) if ahead >= 2 else (0, 1, 2))
                            else:
                                scores(i + 1, t, u1, (0, 1))
                        if t == 0:
                            if later(i, 1):
                                pe.wait_ge(rden_done, i)
                            if ahead >= 2:
                                transpose_x(i + 2)
                            elif ahead:
                                turn_small()
                            else:
                                transpose_chunk(0)
                            pe.wait_ge(m_stacked[u], 32 * (r + 1))
                        if not ahead and t:
                            pe.wait_ge(exp_done, NG * i + t - 1)
                        elif t > 0 or later(i, 1):
                            pe.wait_ge(exp_done, NG * i + t)
                        scores_T(i, t, u)
                        if t > 1 and ahead:
                            scores(i + 1, t, u1, (2,))
                        if t == 0 and ahead >= 2:
                            pe.wait_ge(q_stacked[u1][1], 16 * 3 * (r1 + 1))
                            scores(i + 1, 1, u1, (0,))
                            latents_by_token(i + 2)
                            scores(i + 1, 1, u1, (1,))
                            latents(i + 2)
                        if t == 1 and not ahead:
                            pe.wait_ge(small_done, 1)
                            logits(0, 0)
                        if t == 1 and ahead >= 2:
                            if later(i, 1):
                                pe.wait_ge(o_copied, NG * i)
                            queries(i + 2, 0)
                            pe.wait_ge(lat_lo_done, i + 3)
                            queries(i + 2, 1)
                        if t == 2:
                            if ahead >= 2:
                                pe.wait_ge(q_copied, 2 * i + 5)
                            else:
                                pe.wait_ge(o_copied, NG * i)
                            weigh(i, 0, u, banks[1])
                            if ahead >= 2:
                                pe.wait_ge(q_copied, 2 * i + 6)
                            elif ahead:
                                pe.wait_ge(small_done, 1)
                            else:
                                pe.wait_ge(ms_done, 1)
                            weigh(i, 1, u, banks[0])
                        if t == 3:
                            pe.wait_ge(o_copied, NG * i + 2)
                            if later(i, 1):
                                project(i - 1, banks[0])
                            if ahead:
                                transpose_max(i + 1)
                            weigh(i, 2, u, banks[1])
                    if later(i, 1):
                        pe.wait_ge(x1_done, i)
                    sums(i, u, banks[0])
                    pe.wait_ge(o_copied, NG * i + 3)
                    weigh(i, 3, u, banks[1])
                batches(pe, step)
                pe.wait_ge(exp_done, NG * B)

                def chunk_step(c, r, u, more):
                    if not after(c, 1):
                        pe.wait_ge(w_lo_done, 1)
                    for k in range(HC):
                        up(c, k, u)
                        if k >= LAG:
                            if k == LAG and after(c, 2):
                                pe.wait_ge(yT_done, c - 1)
                            elif k == LAG and after(c, 1):
                                pe.wait_ge(x1_done, B)
                            elif k == LAG:
                                pe.wait_ge(o_copied, NG * B)
                                pe.wait_ge(w_lo_done, 2)
                            down(c, k - LAG, u)
                        elif after(c, 1):
                            down(c - 1, HC + k - LAG, 1 - u)
                        if k == 4 and after(c, 1):
                            turn_y(c - 1)
                        if k == 7 and not after(c, 1):
                            pe.wait_ge(rden_done, B)
                            project(B - 1, banks[0])
                        if more and k == 9:
                            transpose_chunk(c + 1)
                        if more and k == 12:
                            logits(c + 1, 1 - u)
                chunks(pe, chunk_step)
                for k in range(HC - LAG, HC):
                    down(NC - 1, k, 1)
                turn_y(NC - 1)



_INS = ["L0_attn_x_bld", "L0_attn_Wq", "L0_attn_Wkv_down", "L0_attn_Wk_up", "L0_attn_Wv_up", "L0_attn_Wout", "L0_ffn_gate_w",
        "L0_ffn_gate_b", "L0_ffn_rms_w", "L0_ffn_w1", "L0_ffn_b1", "L0_ffn_w2", "L0_ffn_b2"]


def kernel(**inputs):
    import numpy as _np
    import concourse.bacc as _bacc
    from concourse import mybir as _mybir
    from concourse.bass_utils import run_bass_kernel_spmd as _run

    nc = _bacc.Bacc("TRN2", target_bir_lowering=False, num_devices=1)
    arrays, args = {}, []
    for name in _INS:
        a = _np.ascontiguousarray(inputs[name])
        arrays[f"in_{name}"] = a
        args.append(nc.dram_tensor(f"in_{name}", a.shape, _mybir.dt.from_np(a.dtype), kind="ExternalInput").ap())
    shape = inputs["L0_attn_x_bld"].shape
    args.append(nc.dram_tensor("out_0", shape, _mybir.dt.float32, kind="ExternalOutput").ap())
    preln_block(nc, *args)
    r = _run(nc, [arrays], core_ids=[0])
    return r.results[0]["out_0"]
```
